# Optimizing a Trainium2 kernel written in Bass

```python
import numpy as np
import jax
import jax.numpy as jnp

def _softmax(x, axis=-1):
    return jax.nn.softmax(x, axis=axis)
def _gelu(x):
    return jax.nn.gelu(x, approximate=True)
def _silu(x):
    return jax.nn.silu(x)
def _sigmoid(x):
    return jax.nn.sigmoid(x)
def _layernorm(x, axis=-1, eps=1e-5):
    m = jnp.mean(x, axis=axis, keepdims=True)
    v = jnp.var(x, axis=axis, keepdims=True)
    return (x - m) / jnp.sqrt(v + eps)
def _scatter_add(tgt, idx, src, axis=0):
    return tgt.at[idx].add(src)
def _segment_sum(src, seg, n):
    return jax.ops.segment_sum(src, seg, n)

kernel_name = 'mk_conv_preact_d1_conv_nchw256_4ff3ec'

def setup_inputs(seed: int = 0):
    np.random.seed(seed)
    _w = jnp.asarray
    def _rec_inputs():
        import jax
        import jax.numpy as jnp
        _gk = jax.random.key(seed)
        x = -0.0003972 + 0.9999 * jax.random.normal(jax.random.fold_in(_gk, 1), (8, 256, 80, 80), jnp.float32)
        return x
    x = _rec_inputs()
    def _L0_conv_setup():
        import jax, jax.numpy as jnp
        import numpy as np
        RANK = 8
        ALPHA = 16.0
        SCALING = ALPHA / RANK
        K = 3
        STRIDE = (1, 1)
        PAD = ((1, 1), (1, 1))
        IN_CH, OUT_CH = (256, 256)
        B, H, W = (8, 80, 80)

        def _conv(x, w):
            return jax.lax.conv_general_dilated(x, w, window_strides=STRIDE, padding=PAD, dimension_numbers=('NCHW', 'OIHW', 'NCHW'))
        key = jax.random.key(seed)
        k1, k2, k3, k4 = jax.random.split(key, 4)
        x = jax.random.normal(k1, (B, IN_CH, H, W), dtype=jnp.float32)
        W0 = jax.random.normal(k2, (OUT_CH, IN_CH, K, K), dtype=jnp.float32) * 0.02
        lora_A = jax.random.normal(k3, (RANK, IN_CH * K * K), dtype=jnp.float32) / np.sqrt(RANK)
        lora_B = jax.random.normal(k4, (OUT_CH, RANK), dtype=jnp.float32) * 0.02
        return {'x': x, 'W0': W0, 'lora_A': lora_A, 'lora_B': lora_B}
    _L0_conv_all = _L0_conv_setup()
    _L0_conv_in = {k: v for k, v in _L0_conv_all.items() if k in ('W0', 'lora_A', 'lora_B', )}
    del _L0_conv_all

    return {
        "x": x,
        "L0_conv_W0": _L0_conv_in["W0"],
        "L0_conv_lora_A": _L0_conv_in["lora_A"],
        "L0_conv_lora_B": _L0_conv_in["lora_B"],
    }

def reference(x, L0_conv_W0, L0_conv_lora_A, L0_conv_lora_B):
    import jax
    import jax.numpy as jnp
    def _L0_conv_ref(x, W0, lora_A, lora_B):
        import jax, jax.numpy as jnp
        import numpy as np
        RANK = 8
        ALPHA = 16.0
        SCALING = ALPHA / RANK
        K = 3
        STRIDE = (1, 1)
        PAD = ((1, 1), (1, 1))
        IN_CH, OUT_CH = (256, 256)
        B, H, W = (8, 80, 80)

        def _conv(x, w):
            return jax.lax.conv_general_dilated(x, w, window_strides=STRIDE, padding=PAD, dimension_numbers=('NCHW', 'OIHW', 'NCHW'))
        base_out = _conv(x, W0)
        in_ch = x.shape[1]
        A_kern = lora_A.reshape(RANK, in_ch, K, K)
        low = _conv(x, A_kern)
        delta = jnp.einsum('or,brhw->bohw', lora_B, low)
        return base_out + SCALING * delta

    def _gn(v, G=32, eps=1e-5):
        B_, C_, H_, W_ = v.shape
        g = v.reshape(B_, G, C_ // G, H_, W_)
        m = jnp.mean(g, axis=(2, 3, 4), keepdims=True)
        s = jnp.var(g, axis=(2, 3, 4), keepdims=True)
        return ((g - m) / jnp.sqrt(s + eps)).reshape(v.shape)

    def _ln_c(v, eps=1e-6):
        m = jnp.mean(v, axis=1, keepdims=True)
        s = jnp.var(v, axis=1, keepdims=True)
        return (v - m) / jnp.sqrt(s + eps)

    def _ln_t(v, eps=1e-5):
        m = jnp.mean(v, axis=-1, keepdims=True)
        s = jnp.var(v, axis=-1, keepdims=True)
        return (v - m) / jnp.sqrt(s + eps)

    def _to_tokens(v):
        B_, C_, H_, W_ = v.shape
        return v.reshape(B_, C_, H_ * W_).transpose(0, 2, 1)
    def _from_tokens(t, like):
        B_, C_, H_, W_ = like.shape
        return t.transpose(0, 2, 1).reshape(B_, C_, H_, W_)

    x = x + _L0_conv_ref(_gn(x), L0_conv_W0, L0_conv_lora_A, L0_conv_lora_B)
    return x


_drawn_inputs = setup_inputs


def setup_inputs(seed=0):
    import zlib

    import numpy as np

    out = dict(_drawn_inputs(seed))
    spreads = {}
    factors = {}
    for name, (base, spread) in spreads.items():
        noise = np.random.default_rng([zlib.crc32(name.encode()), seed]).standard_normal(out[name].shape)
        drawn = base * np.exp(spread * noise) if base else spread * noise
        out[name] = jnp.asarray(drawn.astype(out[name].dtype))
    for name, factor in factors.items():
        out[name] = (out[name] * factor).astype(out[name].dtype)
    return out
```

```python
from contextlib import ExitStack

import concourse.bass as bass
from concourse import mybir

ALU = mybir.AluOpType
ACT = mybir.ActivationFunctionType
AX_X = mybir.AxisListType.X
F32 = mybir.dt.float32
F16 = mybir.dt.float16
BF16 = mybir.dt.bfloat16
U32 = mybir.dt.uint32

P = 128
NB, CH, H, W = 8, 256, 80, 80
NC = CH // P
TAPS = 3
TILE_ROWS = 4
NJ = TILE_ROWS + TAPS - 1
HALF_ROWS = H // 2
HALF_TILES = HALF_ROWS // TILE_ROWS
SLOT_ROWS = HALF_ROWS + 2
BANK_TILES = 5
NG = HALF_TILES // BANK_TILES
BANK = BANK_TILES * W
PLANE = HALF_TILES * W
RANK = 8
LORA_SCALE = 2.0
GROUP = 8
EPS = 1e-5

PA, PB = 0.75, 1.5
A2, B2 = PA * PA, PB * PB
POINT_NORM = [A2 * B2] + [2 * A2 * (A2 - B2)] * 2 + [2 * B2 * (B2 - A2)] * 2 + [1.0]
PAIRS = [(1, 2), (3, 4), (0, 5)]
NP = len(PAIRS)
IMG_PAIRS = 2 * NP
U_SLOTS = 2
T_RING = 3

X_SCALE = 32.0
W_SCALE = 4096.0

W_ORDER = [(c, j) for pair in PAIRS for c in range(NC) for j in pair]
TRANSFORMED = 2 * 2 * NC

BASES = 2 * NC
ITEMS = 2 * NC
MIX = 20
FINALS = TILE_ROWS * NC
QUANTA = 4
MOMENTS = 3 * QUANTA
LINKS = 30


def build(nc, x, w0t, lora_at, lora_bt, out):
    x_v = x.rearrange("b (c p) h w -> b c p (h w)", p=P)
    out_v = out.rearrange("b (c p) h w -> b c p (h w)", p=P)

    with ExitStack() as ctx:
        def sb(name, shape, dt):
            return ctx.enter_context(nc.sbuf_tensor(name, shape, dt))

        def sem(name):
            return ctx.enter_context(nc.semaphore(name))

        xs = sb("xs", [P, 3, NC, SLOT_ROWS, W], F32)
        w_hi = sb("w_hi", [P, NC, NJ, TAPS, CH], F16)
        w_lo = sb("w_lo", [P, NC, NJ, TAPS, CH], F16)
        u = sb("u", [P, U_SLOTS, 2, 2, NC, HALF_TILES, W + 2], F16)
        common = sb("common", [P, NC, 2, PLANE], F32)
        t_rows = sb("t_rows", [P, T_RING, PLANE], F32)
        prod = sb("prod", [P, NC, 6, PLANE], F32)
        junk = sb("junk", [P, 2, HALF_ROWS // 2 * W], BF16)
        evac_scale = sb("evac_scale", [P, NJ], F32)
        w_ends = sb("w_ends", [P, 2], F32)
        w_ends_all = sb("w_ends_all", [P, 2], F32)
        w_max = sb("w_max", [P, 1], F32)
        w_power = sb("w_power", [P, 1], F32)
        w_inverse = sb("w_inverse", [P, 1], F32)
        w_scale = sb("w_scale", [P, 1], F32)
        sums = sb("sums", [P, NC, 2 * 2], F32)
        squares = sb("squares", [P, NC, 2 * 2], F32)
        neg_shift = sb("neg_shift", [P, NC], F32)
        neg_mean = sb("neg_mean", [P, NC], F32)
        var = sb("var", [P, NC], F32)
        std = sb("std", [P, NC], F32)
        small = sb("small", [P, 12, NC], F32)
        turn_in = sb("turn_in", [P, 32], F32)
        turned = sb("turned", [P, 32], F32)
        grouped = sb("grouped", [P, 4], F32)
        spread = sb("spread", [P, 32], F32)
        turn_out = sb("turn_out", [P, 32], F32)
        row_scale = sb("row_scale", [P, 2, NC], F32)
        bias = sb("bias", [P, 2, 4, NC], F32)
        ps = ctx.enter_context(nc.psum_tensor("ps", [P, 8, 512], F32))
        before = prod[:].rearrange("p c k n -> p (c k n)")
        w_end, a_end = NC * 9 * CH, (NC + 1) * 9 * CH
        w_full = before[:, 0:w_end].rearrange("p (c t n) -> p c t n", c=NC, t=9)
        lora_a = before[0:RANK, w_end:a_end].rearrange("r (t n) -> r t n", t=9)
        lora_b = before[0:RANK, a_end:a_end + CH]

        w_loaded = sem("w_loaded")
        lora_loaded = sem("lora_loaded")
        x_loaded = [[sem(f"x_loaded{s}{c}") for c in range(NC)] for s in range(3)]
        stored = [[sem(f"stored{s}{c}") for c in range(NC)] for s in range(3)]
        pads_zero = sem("pads_zero")
        turn_zero = sem("turn_zero")
        delta_ready = sem("delta_ready")
        merged = sem("merged")
        max_ready = sem("max_ready")
        max_all = sem("max_all")
        scale_step = sem("scale_step")
        scale_ready = sem("scale_ready")
        gbase_ready = sem("gbase_ready")
        g_ready = sem("g_ready")
        whi_ready = sem("whi_ready")
        wlo_ready = sem("wlo_ready")
        shift_sums = sem("shift_sums")
        shift_ready = sem("shift_ready")
        moments_ready = sem("moments_ready")
        stat_step = sem("stat_step")
        mean_ready = sem("mean_ready")
        var_ready = sem("var_ready")
        std_ready = sem("std_ready")
        norm_ready = sem("norm_ready")
        centred = sem("centred")
        base_ready = sem("base_ready")
        t_ready = sem("t_ready")
        hi_ready = sem("hi_ready")
        lo_ready = sem("lo_ready")
        pe_done = sem("pe_done")
        prod_ready = sem("prod_ready")
        mix_ready = sem("mix_ready")
        y_done = sem("y_done")

        def rows(slot, c, k):
            return xs[:, slot, c, k:k + TILE_ROWS * (HALF_TILES - 1) + 1:TILE_ROWS, :]

        def pair_no(i, s):
            return 2 * IMG_PAIRS * i + s

        def half_no(i, s):
            return 4 * i + s // NP

        def at_start(i, s, n):
            return isinstance(i, int) and pair_no(i, s) < n

        def slot_of(s):
            return 0 if s // NP % 2 == 0 else 1 + s // IMG_PAIRS % 2

        def plane(ap):
            return ap.rearrange("p (t w) -> p t w", w=W)

        def g_row(c, kh):
            return w_full[:, c, 3 * kh:3 * kh + 3, :].rearrange("p t n -> p (t n)")

        def g_tile(n):
            c, j = W_ORDER[n]
            if n >= TRANSFORMED:
                return g_row(c, 0 if j == 0 else TAPS - 1)
            tiles = (common[:, 1, 0, :], common[:, 1, 1, :], t_rows[:, 0, :], t_rows[:, 1, :])
            return tiles[n % 4][:, 0:TAPS * CH]

        block = ctx.enter_context(nc.Block())

        @block.sync
        def _(sp):
            def load_top(b, c):
                sp.dma_start(xs[:, 0, c, 1:SLOT_ROWS, :].rearrange("p h w -> p (h w)"),
                             x_v[b, c, :, 0:(HALF_ROWS + 1) * W]).then_inc(x_loaded[0][c], 16)

            def load_bottom(b, par, c):
                sp.dma_start(xs[:, 1 + par, c, 0:SLOT_ROWS - 1, :].rearrange("p h w -> p (h w)"),
                             x_v[b, c, :, (HALF_ROWS - 1) * W:H * W]).then_inc(x_loaded[1 + par][c], 16)

            def store(b, slot, half, c):
                sp.dma_start(out_v[b, c, :, half * HALF_ROWS * W:(half + 1) * HALF_ROWS * W],
                             xs[:, slot, c, 1:HALF_ROWS + 1, :].rearrange("p h w -> p (h w)")
                             ).then_inc(stored[slot][c], 16)

            def images(i, last):
                for par in range(2):
                    b = 2 * i + par
                    more = not (last and par == 1)
                    if more:
                        for c in range(NC):
                            if not (isinstance(i, int) and i + par == 0):
                                sp.wait_ge(stored[2 - par][c], 16 * (i + par))
                            load_bottom(b + 1, 1 - par, c)
                    for c in range(NC):
                        sp.wait_ge(y_done, 2 * FINALS * b + FINALS - 2 + 2 * c)
                        store(b, 0, 0, c)
                    if more:
                        for c in range(NC):
                            sp.wait_ge(stored[0][c], 16 * (b + 1))
                        for c in reversed(range(NC)):
                            load_top(b + 1, c)
                    for c in range(NC):
                        sp.wait_ge(y_done, 2 * FINALS * b + 2 * FINALS - 2 + 2 * c)
                        store(b, 1 + par, 1, c)

            sp.dma_start(lora_a, lora_at).then_inc(lora_loaded, 16)
            sp.dma_start(lora_b, lora_bt).then_inc(lora_loaded, 16)
            sp.dma_start(w_full, w0t.rearrange("(c p) t n -> p c t n", p=P)).then_inc(w_loaded, 16)
            for c in range(NC):
                load_bottom(0, 0, c)
            for c in range(NC):
                load_top(0, c)
            images(0, False)
            with sp.Fori(1, NB // 2 - 1) as i:
                images(i, False)
            images(NB // 2 - 1, True)
            for c in range(NC):
                sp.wait_ge(stored[0][c], 16 * NB)
                for slot in (1, 2):
                    sp.wait_ge(stored[slot][c], 16 * (NB // 2))

        @block.gpsimd
        def _(pool):
            nc.gpsimd.memset(turn_in[:], 0.0).then_inc(turn_zero, 1)
            u_rows = u[:].rearrange("p s k l c t w -> p (s k l c t) w")
            nc.gpsimd.memset(u_rows[:, :, 0:1], 0.0).then_inc(pads_zero, 1)
            nc.gpsimd.memset(u_rows[:, :, W + 1:W + 2], 0.0).then_inc(pads_zero, 1)
            nc.gpsimd.memset(xs[:, 0, :, 0, :], 0.0).then_inc(pads_zero, 1)
            for slot in (1, 2):
                nc.gpsimd.memset(xs[:, slot, :, SLOT_ROWS - 1, :], 0.0).then_inc(pads_zero, 1)
            pool.wait_ge(max_ready, 2)
            nc.gpsimd.partition_all_reduce(w_ends_all[:], w_ends[:], P,
                                           bass.bass_isa.ReduceOp.absmax).then_inc(max_all, 1)

        @block.scalar
        def _(act):
            def unused(b, n):
                if n in (0, 1):
                    if not (isinstance(b, int) and b == 0):
                        act.wait_ge(moments_ready, MOMENTS * b - 1 + n)
                elif n < 6:
                    act.wait_ge(shift_sums, QUANTA * b + n - 1)
                else:
                    act.wait_ge(moments_ready, MOMENTS * b + n - 5)
                return junk[:, n % 2, :]

            def quarter(slot, c, p):
                return xs[:, slot, c, 1 + HALF_ROWS // 2 * p:1 + HALF_ROWS // 2 * (p + 1), :].rearrange(
                    "p h w -> p (h w)")

            def bottom_sum(b, par, loads, c, p):
                if p == 0:
                    act.wait_ge(x_loaded[1 + par][c], 16 * loads)
                nc.scalar.activation(unused(b, 2 * c + p), quarter(1 + par, c, p), ACT.Identity,
                                     accum_out=sums[:, c, p:p + 1]).then_inc(shift_sums, 1)

            def bottom_square(b, par, c, p):
                nc.scalar.activation(unused(b, 4 + 2 * c + p), quarter(1 + par, c, p), ACT.Square,
                                     bias=neg_shift[:, c:c + 1],
                                     accum_out=squares[:, c, p:p + 1]).then_inc(moments_ready, 1)

            def top_sum(b, c, p):
                if p == 0:
                    act.wait_ge(x_loaded[0][c], 16 * (b + 1))
                nc.scalar.activation(unused(b, 8 + 2 * c + p), quarter(0, c, p), ACT.Identity,
                                     accum_out=sums[:, c, 2 + p:3 + p]).then_inc(moments_ready, 1)

            def top_square(b, c, p):
                nc.scalar.activation(unused(b, 12 + 2 * c + p), quarter(0, c, p), ACT.Square,
                                     bias=neg_shift[:, c:c + 1],
                                     accum_out=squares[:, c, 2 + p:3 + p]).then_inc(moments_ready, 1)

            def centre(slot, c, p):
                r0 = (1 if slot == 0 else 0) + 21 * p
                part = xs[:, slot, c, r0:r0 + 21 - p, :]
                nc.scalar.activation(part, part, ACT.Identity, bias=neg_mean[:, c:c + 1]
                                     ).then_inc(centred, 1)

            def take_root(b):
                act.wait_ge(var_ready, b + 1)
                nc.scalar.activation(std[:], var[:], ACT.Sqrt).then_inc(std_ready, 1)

            def round_hi(i, s, n):
                c, k = n // 2, n % 2
                act.wait_ge(t_ready, ITEMS * pair_no(i, s) + n + 1)
                t = t_rows[:, (ITEMS * s + n) % T_RING, :]
                nc.scalar.activation(u[:, s % U_SLOTS, k, 0, c, :, 1:W + 1], plane(t), ACT.Identity,
                                     scale=row_scale[:, s // IMG_PAIRS % 2, c:c + 1]).then_inc(hi_ready, 1)

            def evacuate(i, s, k):
                par, pair, j = s // IMG_PAIRS % 2, s % NP, PAIRS[s % NP][k]
                dest = {1: 0, 2: 1, 3: 3, 4: 4, 0: 3, 5: 5}[j]
                bias_at = {1: 0, 2: 1, 0: 2, 5: 3}.get(j)
                first = at_start(i, s, NP)
                half = half_no(i, s)
                for co in range(NC):
                    if co == 0:
                        if pair == 0 and not first:
                            act.wait_ge(mix_ready, MIX * half - (4 if k == 0 else 0))
                        if pair == 1 and k == 0 and not first:
                            act.wait_ge(y_done, FINALS * half)
                        if pair == 2:
                            act.wait_ge(y_done, FINALS * half + 2 + 2 * k)
                    act.wait_ge(pe_done, ITEMS * pair_no(i, s) + NC * k + co + 1)
                    src = ps[:, 4 * k + 2 * co:4 * k + 2 * co + 2, 0:BANK]
                    dst = prod[:, co, dest, :].rearrange("p (g n) -> p g n", g=NG)
                    if bias_at is None:
                        nc.scalar.activation(dst, src, ACT.Identity, scale=evac_scale[:, j:j + 1]
                                             ).then_inc(prod_ready, 1)
                    else:
                        nc.scalar.activation(dst, src, ACT.Identity, scale=evac_scale[:, j:j + 1],
                                             bias=bias[:, par, bias_at, co:co + 1]
                                             ).then_inc(prod_ready, 1)

            def step(i, s, rounds, stats):
                q, par = s % IMG_PAIRS, s // IMG_PAIRS % 2
                b = 2 * i + s // IMG_PAIRS
                quarters = [(c, p) for c in range(NC) for p in range(2)]
                extra = []
                if q == 0:
                    extra = [lambda c=c, p=p: centre(1 + par, c, p) for c, p in quarters]
                if stats and q == 1:
                    extra = [lambda c=c, p=p: bottom_sum(b + 1, 1 - par, i + 1 + par, c, p) for c, p in quarters]
                if stats and q == 3:
                    act.wait_ge(shift_ready, b + 2)
                    extra = [lambda c=c, p=p: bottom_square(b + 1, 1 - par, c, p) for c, p in quarters]
                if stats and q == 4:
                    extra = [lambda c=c, p=p: top_sum(b + 1, c, p) for c, p in quarters]
                    extra += [lambda c=c, p=p: top_square(b + 1, c, p) for c, p in quarters]
                if not at_start(i, s, 1):
                    evacuate(i, s - 1, 1)
                if stats and q == 5:
                    take_root(b + 1)
                    act.wait_ge(mean_ready, b + 2)
                    for c, p in quarters:
                        centre(0, c, p)
                    act.wait_ge(norm_ready, b + 2)
                for n in range(ITEMS):
                    if rounds:
                        round_hi(i, s + 1, n)
                    if extra:
                        extra.pop(0)()
                evacuate(i, s, 0)
                while extra:
                    extra.pop(0)()

            quarters = [(c, p) for c in range(NC) for p in range(2)]

            def round_w(n):
                c, j = W_ORDER[n]
                if n < TRANSFORMED:
                    act.wait_ge(g_ready, n + 1)
                nc.scalar.activation(w_hi[:, c, j, :, :].rearrange("p t n -> p (t n)"), g_tile(n),
                                     ACT.Identity, scale=w_scale[:]).then_inc(whi_ready, 1)

            for c, p in quarters:
                bottom_sum(0, 0, 1, c, p)
            act.wait_ge(shift_ready, 1)
            for c, p in quarters:
                bottom_square(0, 0, c, p)
            for c, p in quarters:
                top_sum(0, c, p)
            for c, p in quarters:
                top_square(0, c, p)
            act.wait_ge(scale_ready, 1)
            for n in range(len(W_ORDER)):
                round_w(n)
            take_root(0)
            act.wait_ge(mean_ready, 1)
            for c, p in quarters:
                centre(0, c, p)
            act.wait_ge(norm_ready, 1)
            for n in range(ITEMS):
                round_hi(0, 0, n)
            step(0, 0, True, True)
            with act.Fori(0, NB // 2 - 1) as i:
                for s in range(1, 13):
                    step(i, s, True, True)
            for s in range(1, 12):
                step(NB // 2 - 1, s, s < 11, s < IMG_PAIRS)
            evacuate(NB // 2 - 1, 2 * IMG_PAIRS - 1, 1)

        @block.vector
        def _(dve):
            linked = [0]

            def link(b, ins):
                linked[0] += 1
                ins.then_inc(stat_step, 1)
                dve.wait_ge(stat_step, LINKS * b + linked[0])

            def sm(n):
                return small[:, n, :]

            def shift(b):
                linked[0] = 0
                dve.wait_ge(shift_sums, QUANTA * (b + 1))
                link(b, nc.vector.tensor_tensor(sm(0), sums[:, :, 0], sums[:, :, 1], ALU.add))
                nc.vector.tensor_scalar(neg_shift[:], sm(0), -1.0 / (HALF_ROWS * W), None, ALU.mult
                                        ).then_inc(shift_ready, 1)

            def group_mean(b, src, dst):
                link(b, nc.vector.tensor_copy(turn_in[:, 0:NC], src))
                link(b, nc.vector.transpose(turned[:], turn_in[:]))
                link(b, nc.vector.tensor_reduce(grouped[:], turned[:].rearrange("p (g n) -> p g n", n=GROUP),
                                                AX_X, ALU.add))
                link(b, nc.vector.tensor_scalar(spread[:].rearrange("p (g n) -> p g n", n=GROUP),
                                                grouped[:, :, None].to_broadcast([P, 4, GROUP]),
                                                1.0 / GROUP, None, ALU.mult))
                link(b, nc.vector.transpose(turn_out[:], spread[:]))
                link(b, nc.vector.tensor_copy(dst, turn_out[:, 0:NC]))

            def statistics(b, par):
                dve.wait_ge(moments_ready, MOMENTS * (b + 1))
                link(b, nc.vector.tensor_reduce(sm(0), sums[:], AX_X, ALU.add))
                link(b, nc.vector.tensor_reduce(sm(1), squares[:], AX_X, ALU.add))
                link(b, nc.vector.tensor_scalar(sm(2), sm(0), 1.0 / (H * W), None, ALU.mult))
                link(b, nc.vector.tensor_tensor(sm(3), sm(2), neg_shift[:], ALU.add))
                link(b, nc.vector.tensor_tensor(sm(4), sm(3), sm(3), ALU.mult))
                link(b, nc.vector.scalar_tensor_tensor(out=sm(5), in0=sm(1), scalar=1.0 / (H * W), in1=sm(4),
                                                       op0=ALU.mult, op1=ALU.subtract))
                group_mean(b, sm(2), sm(6))
                nc.vector.tensor_scalar(neg_mean[:], sm(6), -1.0, None, ALU.mult).then_inc(mean_ready, 1)
                link(b, nc.vector.tensor_tensor(sm(7), sm(2), sm(6), ALU.subtract))
                link(b, nc.vector.tensor_tensor(sm(8), sm(7), sm(7), ALU.mult))
                link(b, nc.vector.tensor_tensor(sm(9), sm(8), sm(5), ALU.add))
                group_mean(b, sm(9), sm(10))
                nc.vector.tensor_scalar(var[:], sm(10), EPS, None, ALU.add).then_inc(var_ready, 1)
                for n, share in enumerate(((1 / A2 + 1 / PA) / 2, (1 / A2 - 1 / PA) / 2, 1 - 1 / A2, 1 - A2)):
                    link(b, nc.vector.tensor_scalar(bias[:, par, n, :], sm(6), share, None, ALU.mult))
                dve.wait_ge(std_ready, b + 1)
                link(b, nc.vector.reciprocal(sm(0), std[:]))
                link(b, nc.vector.tensor_tensor(sm(1), sm(0), sm(0), ALU.mult))
                link(b, nc.vector.tensor_tensor(sm(3), sm(1), var[:], ALU.mult))
                link(b, nc.vector.tensor_scalar(sm(4), sm(3), -0.5 * X_SCALE, 1.5 * X_SCALE, ALU.mult, ALU.add))
                nc.vector.tensor_tensor(row_scale[:, par, :], sm(0), sm(4), ALU.mult).then_inc(norm_ready, 1)
                assert linked[0] == LINKS, linked[0]

            def base(i, s, c):
                slot, pair = slot_of(s), s % NP
                if c == 0 and at_start(i, s, 1):
                    dve.wait_ge(pads_zero, 5)
                    dve.wait_ge(wlo_ready, NC * NJ)
                if pair == 0:
                    dve.wait_ge(centred, QUANTA * half_no(i, s) + 2 * c + 2)
                if not at_start(i, s, 1):
                    dve.wait_ge(t_ready, ITEMS * (pair_no(i, s) - 1) + 2 * c + 2)
                d = [rows(slot, c, k) for k in range(NJ)]
                near = -(A2 + B2)
                terms = [((d[2], -B2, d[4]), (d[1], -B2, d[3])),
                         ((d[2], -A2, d[4]), (d[1], -A2, d[3])),
                         ((d[2], near, d[4]), (d[3], near, d[5]))][pair]
                for n, (in0, scalar, in1) in enumerate(terms):
                    nc.vector.scalar_tensor_tensor(out=plane(common[:, c, n, :]), in0=in0, scalar=scalar, in1=in1,
                                                   op0=ALU.mult, op1=ALU.add).then_inc(base_ready, 1)

            def transform(i, s, c, k):
                slot, pair, n = slot_of(s), s % NP, 2 * c + k
                t = plane(t_rows[:, (ITEMS * s + n) % T_RING, :])
                dve.wait_ge(base_ready, BASES * pair_no(i, s) + 2 * c + 2)
                if not at_start(i, s, 1) or n >= T_RING:
                    dve.wait_ge(lo_ready, ITEMS * pair_no(i, s) + n - T_RING + 1)
                if pair < 2:
                    p = (PA, PB)[pair] * (1 - 2 * k)
                    in0, scalar, in1 = plane(common[:, c, 1, :]), p, plane(common[:, c, 0, :])
                else:
                    in0, scalar, in1 = rows(slot, c, k), A2 * B2, plane(common[:, c, k, :])
                nc.vector.scalar_tensor_tensor(out=t, in0=in0, scalar=scalar, in1=in1,
                                               op0=ALU.mult, op1=ALU.add).then_inc(t_ready, 1)

            def round_lo(i, s, n):
                c, k = n // 2, n % 2
                t = plane(t_rows[:, (ITEMS * s + n) % T_RING, :])
                dve.wait_ge(hi_ready, ITEMS * pair_no(i, s) + n + 1)
                nc.vector.scalar_tensor_tensor(out=u[:, s % U_SLOTS, k, 1, c, :, 1:W + 1], in0=t,
                                               scalar=row_scale[:, s // IMG_PAIRS % 2, c:c + 1],
                                               in1=u[:, s % U_SLOTS, k, 0, c, :, 1:W + 1],
                                               op0=ALU.mult, op1=ALU.subtract).then_inc(lo_ready, 1)

            def transform_pair(i, s):
                for c in range(NC):
                    base(i, s, c)
                transform(i, s, 0, 0)
                transform(i, s, 0, 1)
                transform(i, s, 1, 0)
                round_lo(i, s, 0)
                round_lo(i, s, 1)
                transform(i, s, 1, 1)
                round_lo(i, s, 2)
                round_lo(i, s, 3)

            def combine(i, s):
                slot, pair, half = slot_of(s), s % NP, half_no(i, s)
                M = [[prod[:, co, k, :] for k in range(6)] for co in range(NC)]

                def mixed(n):
                    dve.wait_ge(mix_ready, MIX * half + n)

                def stt(out, in0, scalar, in1):
                    return nc.vector.scalar_tensor_tensor(out=out, in0=in0, scalar=scalar, in1=in1,
                                                          op0=ALU.mult, op1=ALU.add)

                def finish(row, co, scalar, src):
                    y = rows(slot, co, 1 + row)
                    if scalar is None:
                        ins = nc.vector.tensor_tensor(y, plane(src), y, ALU.add)
                    else:
                        ins = stt(y, plane(src), scalar, y)
                    ins.then_inc(y_done, 1)

                def both(out, k0, k1, op):
                    for co in range(NC):
                        nc.vector.tensor_tensor(M[co][out], M[co][k0], M[co][k1], op).then_inc(mix_ready, 1)

                dve.wait_ge(prod_ready, ITEMS * (pair_no(i, s) + 1))
                if pair == 0:
                    if not at_start(i, s, NP):
                        mixed(0)
                    both(2, 0, 1, ALU.add)
                    for co in range(NC):
                        mixed(1 + co)
                        nc.vector.tensor_tensor(M[co][1], M[co][0], M[co][1], ALU.subtract).then_inc(mix_ready, 1)
                if pair == 1:
                    mixed(4)
                    both(0, 3, 4, ALU.add)
                    for co in range(NC):
                        mixed(5 + co)
                        nc.vector.tensor_tensor(M[co][4], M[co][3], M[co][4], ALU.subtract).then_inc(mix_ready, 1)
                    for co in range(NC):
                        mixed(7 + co)
                        stt(M[co][3], M[co][4], PB / PA, M[co][1]).then_inc(mix_ready, 1)
                    if not at_start(i, s, NP):
                        dve.wait_ge(y_done, FINALS * half)
                    for co in range(NC):
                        stt(M[co][5], M[co][0], (PB / PA) ** 2, M[co][2]).then_inc(mix_ready, 1)
                    dve.wait_ge(t_ready, ITEMS * NP * (half + 1))
                    for co in range(NC):
                        mixed(9 + co)
                        finish(1, co, PA, M[co][3])
                    for co in range(NC):
                        mixed(11 + co)
                        finish(2, co, A2, M[co][5])
                if pair == 2:
                    mixed(12)
                    for co in range(NC):
                        stt(M[co][1], M[co][4], (PB / PA) ** 3, M[co][1]).then_inc(mix_ready, 1)
                    both(2, 0, 2, ALU.add)
                    for co in range(NC):
                        mixed(15 + co)
                        nc.vector.tensor_tensor(M[co][3], M[co][2], M[co][3], ALU.add).then_inc(mix_ready, 1)
                        stt(M[co][5], M[co][1], PA ** 3, M[co][5]).then_inc(mix_ready, 1)
                    for co in range(NC):
                        mixed(17 + 2 * co)
                        finish(0, co, None, M[co][3])
                        mixed(18 + 2 * co)
                        finish(3, co, None, M[co][5])

            def step(i, s, more, stats):
                q, par, b = s % IMG_PAIRS, s // IMG_PAIRS % 2, 2 * i + s // IMG_PAIRS
                if stats and q == 5:
                    statistics(b + 1, 1 - par)
                if not at_start(i, s, 1):
                    combine(i, s - 1)
                if stats and q == 2:
                    shift(b + 1)
                if more:
                    transform_pair(i, s + 1)

            dve.wait_ge(w_loaded, 16)
            for n in range(2 * 5):
                c, m = n // 5, n % 5
                dve.wait_ge(delta_ready, n + 1)
                part = w_full[:, c, 2 * m:min(2 * m + 2, 9), :].rearrange("p t n -> p (t n)")
                nc.vector.scalar_tensor_tensor(out=part, in0=ps[:, n % 8, 0:part.shape[1]], scalar=LORA_SCALE,
                                               in1=part, op0=ALU.mult, op1=ALU.add).then_inc(merged, 1)
            dve.wait_ge(merged, 10)
            for n, end in enumerate((ALU.max, ALU.min)):
                nc.vector.tensor_reduce(w_ends[:, n:n + 1], w_full.rearrange("p c t n -> p (c t n)"), AX_X, end
                                        ).then_inc(max_ready, 1)
            dve.wait_ge(max_all, 1)
            nc.vector.scalar_tensor_tensor(out=w_max[:], in0=w_ends_all[:, 0:1], scalar=1e-30,
                                           in1=w_ends_all[:, 1:2], op0=ALU.max, op1=ALU.max
                                           ).then_inc(scale_step, 1)
            dve.wait_ge(scale_step, 1)
            nc.vector.tensor_scalar(w_power[:].bitcast(U32), w_max[:].bitcast(U32), 0x7F800000, None,
                                    ALU.bitwise_and).then_inc(scale_step, 1)
            dve.wait_ge(scale_step, 2)
            nc.vector.reciprocal(w_inverse[:], w_power[:]).then_inc(scale_step, 1)
            for j in range(NJ):
                nc.vector.tensor_scalar(evac_scale[:, j:j + 1], w_power[:],
                                        1.0 / (W_SCALE * X_SCALE * POINT_NORM[j]), None, ALU.mult
                                        ).then_inc(scale_step, 1)
            dve.wait_ge(scale_step, 3)
            nc.vector.tensor_scalar(w_scale[:], w_inverse[:], W_SCALE, None, ALU.mult
                                    ).then_inc(scale_ready, 1)

            def lo_w(n):
                c, j = W_ORDER[n]
                dve.wait_ge(whi_ready, n + 1)
                hi = w_hi[:, c, j, :, :].rearrange("p t n -> p (t n)")
                nc.vector.scalar_tensor_tensor(out=w_lo[:, c, j, :, :].rearrange("p t n -> p (t n)"), in0=g_tile(n),
                                               scalar=w_scale[:], in1=hi, op0=ALU.mult,
                                               op1=ALU.subtract).then_inc(wlo_ready, 1)

            shift(0)
            dve.wait_ge(scale_ready, 1)
            for m in range(TRANSFORMED // 2):
                c, p = m % 2, (PA, PB)[m // 2]
                even = common[:, 0, m % 2, 0:TAPS * CH]
                if m >= 2:
                    dve.wait_ge(g_ready, 2 * m - 2)
                nc.vector.scalar_tensor_tensor(out=even, in0=g_row(c, 2), scalar=p * p, in1=g_row(c, 0),
                                               op0=ALU.mult, op1=ALU.add).then_inc(gbase_ready, 1)
                if m:
                    lo_w(2 * m - 2)
                    lo_w(2 * m - 1)
                dve.wait_ge(gbase_ready, m + 1)
                for k in range(2):
                    if m >= 2:
                        dve.wait_ge(wlo_ready, 2 * m + k - 3)
                    nc.vector.scalar_tensor_tensor(out=g_tile(2 * m + k), in0=g_row(c, 1),
                                                   scalar=p * (1 - 2 * k), in1=even,
                                                   op0=ALU.mult, op1=ALU.add).then_inc(g_ready, 1)
            for n in range(6, len(W_ORDER)):
                lo_w(n)

            statistics(0, 0)
            transform_pair(0, 0)
            step(0, 0, True, True)
            with dve.Fori(0, NB // 2 - 1) as i:
                for s in range(1, 13):
                    step(i, s, True, True)
            for s in range(1, 13):
                step(NB // 2 - 1, s, s < 11, s < IMG_PAIRS)

        @block.tensor
        def _(pe):
            pe.wait_ge(lora_loaded, 32)
            for n in range(10):
                c, m = n // 5, n % 5
                if n >= 8:
                    pe.wait_ge(merged, n - 7)
                for tap in range(2 * m, min(2 * m + 2, 9)):
                    mm = nc.tensor.matmul(ps[:, n % 8, (tap % 2) * CH:(tap % 2 + 1) * CH],
                                          lora_a[:, tap, c * P:(c + 1) * P], lora_b, start=True, stop=True)
                mm.then_inc(delta_ready, 1)

            pe.wait_ge(wlo_ready, NC * NJ)
            pe.wait_ge(pads_zero, 5)

            def multiply(Q, s):
                for k in range(2):
                    pe.wait_ge(lo_ready, ITEMS * Q + 3 + k)
                    for co in range(NC):
                        if not (isinstance(Q, int) and Q == 0):
                            pe.wait_ge(prod_ready, ITEMS * (Q - 1) + NC * k + co + 1)
                        terms = [(w, hl, ci, kw) for w, hl in ((w_hi, 0), (w_lo, 0), (w_hi, 1))
                                 for ci in range(NC) for kw in range(TAPS)]
                        for n, (w, hl, ci, kw) in enumerate(terms):
                            for g in range(NG):
                                mm = nc.tensor.matmul(
                                    plane(ps[:, 4 * k + 2 * co + g, 0:BANK]),
                                    w[:, ci, PAIRS[s % NP][k], kw, co * P:(co + 1) * P],
                                    u[:, s % U_SLOTS, k, hl, ci, g * BANK_TILES:(g + 1) * BANK_TILES, kw:kw + W],
                                    start=(n == 0), stop=(n == len(terms) - 1))
                        mm.then_inc(pe_done, 1)

            for s in range(IMG_PAIRS):
                multiply(s, s)
            with pe.Fori(1, NB) as b:
                for s in range(IMG_PAIRS):
                    multiply(IMG_PAIRS * b + s, s)


def kernel(x, L0_conv_W0, L0_conv_lora_A, L0_conv_lora_B):
    import numpy as np
    import concourse.bacc as bacc
    from concourse import mybir as mb
    from concourse.bass_utils import run_bass_kernel_spmd

    x = np.ascontiguousarray(x)
    w0t = np.ascontiguousarray(np.asarray(L0_conv_W0).transpose(1, 2, 3, 0).reshape(CH, 9, CH))
    lora_at = np.ascontiguousarray(np.asarray(L0_conv_lora_A).reshape(RANK, CH, 9).transpose(0, 2, 1))
    lora_bt = np.ascontiguousarray(np.asarray(L0_conv_lora_B).T)
    arrays = {"x_dram": x, "w0t_dram": w0t, "lora_at_dram": lora_at, "lora_bt_dram": lora_bt}
    nc = bacc.Bacc("TRN2", target_bir_lowering=False, num_devices=1)
    args = [nc.dram_tensor(name, a.shape, mb.dt.from_np(a.dtype), kind="ExternalInput").ap()
            for name, a in arrays.items()]
    out = nc.dram_tensor("out_dram", x.shape, mb.dt.from_np(x.dtype), kind="ExternalOutput").ap()
    build(nc, *args, out)
    r = run_bass_kernel_spmd(nc, [arrays], core_ids=[0])
    return r.results[0]["out_dram"]
```

```python
from contextlib import ExitStack

import concourse.bass as bass
from concourse import mybir

ALU = mybir.AluOpType
ACT = mybir.ActivationFunctionType
AX_X = mybir.AxisListType.X
F32 = mybir.dt.float32
F16 = mybir.dt.float16
BF16 = mybir.dt.bfloat16
U32 = mybir.dt.uint32

P = 128
NB, CH, H, W = 8, 256, 80, 80
NC = CH // P
TAPS = 3
TILE_ROWS = 4
NJ = TILE_ROWS + TAPS - 1
HALF_ROWS = H // 2
HALF_TILES = HALF_ROWS // TILE_ROWS
SLOT_ROWS = HALF_ROWS + 2
BANK_TILES = 5
NG = HALF_TILES // BANK_TILES
BANK = BANK_TILES * W
PLANE = HALF_TILES * W
RANK = 8
LORA_SCALE = 2.0
GROUP = 8
EPS = 1e-5

PA, PB = 0.75, 1.5
A2, B2 = PA * PA, PB * PB
POINT_NORM = [A2 * B2] + [2 * A2 * (A2 - B2)] * 2 + [2 * B2 * (B2 - A2)] * 2 + [1.0]
PAIRS = [(1, 2), (3, 4), (0, 5)]
NP = len(PAIRS)
IMG_PAIRS = 2 * NP
U_SLOTS = 2

X_SCALE = 32.0
W_SCALE = 4096.0

W_ORDER = [(c, j) for pair in PAIRS for c in range(NC) for j in pair]
TRANSFORMED = 2 * 2 * NC

PRODS = 2 * NC
MIX = 10
FINALS = 6
QUANTA = 4
MOMENTS = 3 * QUANTA
STEPS = 22


def build(nc, x, w0t, lora_at, lora_bt, out):
    x_v = x.rearrange("b (c p) h w -> b c p (h w)", p=P)
    out_v = out.rearrange("b (c p) h w -> b c p (h w)", p=P)

    with ExitStack() as ctx:
        def sb(name, shape, dt):
            return ctx.enter_context(nc.sbuf_tensor(name, shape, dt))

        def sem(name):
            return ctx.enter_context(nc.semaphore(name))

        xs = sb("xs", [P, 3, NC, SLOT_ROWS, W], F32)
        w_hi = sb("w_hi", [P, NC, NJ, TAPS, CH], F16)
        w_lo = sb("w_lo", [P, NC, NJ, TAPS, CH], F16)
        u = sb("u", [P, U_SLOTS, NC, 2, HALF_TILES, 2, W + 2], F16)
        common = sb("common", [P, NC, HALF_TILES, 2, W], F32)
        t_rows = sb("t_rows", [P, NC, HALF_TILES, 2, W], F32)
        prod = sb("prod", [P, NC, 6, PLANE], F32)
        junk = sb("junk", [P, HALF_ROWS // 2 * W], BF16)
        evac_scale = sb("evac_scale", [P, NJ], F32)
        w_ends = sb("w_ends", [P, 2 * NC], F32)
        w_ends_all = sb("w_ends_all", [P, 2 * NC], F32)
        w_max = sb("w_max", [P, 1], F32)
        w_floor = sb("w_floor", [P, 1], F32)
        w_power = sb("w_power", [P, 1], F32)
        w_inverse = sb("w_inverse", [P, 1], F32)
        w_scale = sb("w_scale", [P, 1], F32)
        sums = sb("sums", [P, NC, 2 * 2], F32)
        squares = sb("squares", [P, NC, 2 * 2], F32)
        neg_shift = sb("neg_shift", [P, NC], F32)
        neg_mean = sb("neg_mean", [P, NC], F32)
        var = sb("var", [P, NC], F32)
        std = sb("std", [P, NC], F32)
        small = sb("small", [P, 7, NC], F32)
        turn_in = sb("turn_in", [P, 32], F32)
        turned = sb("turned", [P, 32], F32)
        grouped = sb("grouped", [P, 4], F32)
        spread = sb("spread", [P, 32], F32)
        turn_out = sb("turn_out", [P, 32], F32)
        row_scale = sb("row_scale", [P, 2, NC], F32)
        bias = sb("bias", [P, 2, 4, NC], F32)
        ps = ctx.enter_context(nc.psum_tensor("ps", [P, 8, 512], F32))
        w_full = xs[:, 2].rearrange("p c h w -> p (c h w)")[:, 0:NC * 9 * CH].rearrange(
            "p (c t n) -> p c t n", c=NC, t=9)
        lora = t_rows[0:RANK].rearrange("r c t k w -> r (c t k w)")
        lora_a = lora[:, 0:9 * CH].rearrange("r (t n) -> r t n", t=9)
        lora_b = lora[:, 9 * CH:10 * CH]

        w_loaded = [sem(f"w_loaded{c}") for c in range(NC)]
        lora_loaded = sem("lora_loaded")
        x_loaded = [[sem(f"x_loaded{s}{c}") for c in range(NC)] for s in range(3)]
        stored = [[sem(f"stored{s}{c}") for c in range(NC)] for s in range(3)]
        pads_zero = sem("pads_zero")
        last_pad_zero = sem("last_pad_zero")
        turn_zero = sem("turn_zero")
        delta_ready = sem("delta_ready")
        merged = sem("merged")
        max_ready = sem("max_ready")
        max_all = sem("max_all")
        scale_step = sem("scale_step")
        scale_ready = sem("scale_ready")
        gbase_ready = sem("gbase_ready")
        g_ready = sem("g_ready")
        whi_ready = sem("whi_ready")
        wlo_ready = sem("wlo_ready")
        shift_sums = sem("shift_sums")
        shift_ready = sem("shift_ready")
        moments_ready = sem("moments_ready")
        stat_step = sem("stat_step")
        mean_ready = sem("mean_ready")
        var_ready = sem("var_ready")
        std_ready = sem("std_ready")
        norm_ready = sem("norm_ready")
        centred = sem("centred")
        base_ready = sem("base_ready")
        t_ready = sem("t_ready")
        hi_ready = sem("hi_ready")
        lo_ready = sem("lo_ready")
        pe_done = sem("pe_done")
        prod_ready = sem("prod_ready")
        mix_ready = sem("mix_ready")
        y_done = sem("y_done")

        def rows(slot, c, k):
            return xs[:, slot, c, k:k + TILE_ROWS * (HALF_TILES - 1) + 1:TILE_ROWS, :]

        def two_rows(slot, c, k):
            start = 0 if k < 2 else 2
            tiles = xs[:, slot, c, start:start + HALF_ROWS, :].rearrange("p (t r) w -> p t r w", r=TILE_ROWS)
            return tiles[:, :, k - start:k - start + 2, :].rearrange("p t r w -> p t (r w)")

        def stacked(ap):
            return ap.rearrange("p t k w -> p (t k) w")

        def pair_no(i, s):
            return 2 * IMG_PAIRS * i + s

        def half_no(i, s):
            return 4 * i + s // NP

        def at_start(i, s, n):
            return isinstance(i, int) and pair_no(i, s) < n

        def slot_of(s):
            return 0 if s // NP % 2 == 0 else 1 + s // IMG_PAIRS % 2

        def plane(ap):
            return ap.rearrange("p (t w) -> p t w", w=W)

        def g_row(c, kh):
            return w_full[:, c, 3 * kh:3 * kh + 3, :].rearrange("p t n -> p (t n)")

        def g_tile(n):
            c, j = W_ORDER[n]
            if n >= TRANSFORMED:
                return g_row(c, 0 if j == 0 else TAPS - 1)
            return prod[:, n // 2 % 2, 3 + n % 2, 0:TAPS * CH]

        block = ctx.enter_context(nc.Block())

        @block.sync
        def _(sp):
            def load_top(b, c):
                sp.dma_start(xs[:, 0, c, 1:SLOT_ROWS, :].rearrange("p h w -> p (h w)"),
                             x_v[b, c, :, 0:(HALF_ROWS + 1) * W]).then_inc(x_loaded[0][c], 16)

            def load_bottom(b, par, c):
                sp.dma_start(xs[:, 1 + par, c, 0:SLOT_ROWS - 1, :].rearrange("p h w -> p (h w)"),
                             x_v[b, c, :, (HALF_ROWS - 1) * W:H * W]).then_inc(x_loaded[1 + par][c], 16)

            def store(b, slot, half, c):
                sp.dma_start(out_v[b, c, :, half * HALF_ROWS * W:(half + 1) * HALF_ROWS * W],
                             xs[:, slot, c, 1:HALF_ROWS + 1, :].rearrange("p h w -> p (h w)")
                             ).then_inc(stored[slot][c], 16)

            def images(i, last):
                for par in range(2):
                    b = 2 * i + par
                    more = not (last and par == 1)
                    if more:
                        for c in range(NC):
                            if not (isinstance(i, int) and i + par == 0):
                                sp.wait_ge(stored[2 - par][c], 16 * (i + par))
                            else:
                                sp.wait_ge(wlo_ready, NC * NJ)
                            load_bottom(b + 1, 1 - par, c)
                    sp.wait_ge(y_done, 2 * FINALS * b + FINALS)
                    for c in range(NC):
                        store(b, 0, 0, c)
                    if more:
                        for c in range(NC):
                            sp.wait_ge(stored[0][c], 16 * (b + 1))
                        for c in reversed(range(NC)):
                            load_top(b + 1, c)
                    sp.wait_ge(y_done, 2 * FINALS * b + 2 * FINALS)
                    for c in range(NC):
                        store(b, 1 + par, 1, c)

            sp.dma_start(lora_a, lora_at).then_inc(lora_loaded, 16)
            sp.dma_start(lora_b, lora_bt).then_inc(lora_loaded, 16)
            load_bottom(0, 0, 0)
            for c in range(NC):
                sp.dma_start(w_full[:, c], w0t[c * P:(c + 1) * P]).then_inc(w_loaded[c], 16)
            load_bottom(0, 0, 1)
            for c in range(NC):
                load_top(0, c)
            images(0, False)
            with sp.Fori(1, NB // 2 - 1) as i:
                images(i, False)
            images(NB // 2 - 1, True)
            for c in range(NC):
                sp.wait_ge(stored[0][c], 16 * NB)
                for slot in (1, 2):
                    sp.wait_ge(stored[slot][c], 16 * (NB // 2))

        @block.gpsimd
        def _(pool):
            nc.gpsimd.memset(turn_in[:], 0.0).then_inc(turn_zero, 1)
            u_rows = u[:].rearrange("p s c l t k w -> p (s c l t k) w")
            nc.gpsimd.memset(u_rows[:, :, 0:1], 0.0).then_inc(pads_zero, 1)
            nc.gpsimd.memset(u_rows[:, :, W + 1:W + 2], 0.0).then_inc(pads_zero, 1)
            nc.gpsimd.memset(xs[:, 0, :, 0, :], 0.0).then_inc(pads_zero, 1)
            nc.gpsimd.memset(xs[:, 1, :, SLOT_ROWS - 1, :], 0.0).then_inc(pads_zero, 1)
            pool.wait_ge(max_ready, 2 * NC)
            nc.gpsimd.partition_all_reduce(w_ends_all[:], w_ends[:], P,
                                           bass.bass_isa.ReduceOp.absmax).then_inc(max_all, 1)
            pool.wait_ge(wlo_ready, NC * NJ)
            nc.gpsimd.memset(xs[:, 2, :, SLOT_ROWS - 1, :], 0.0).then_inc(last_pad_zero, 1)

        @block.scalar
        def _(act):
            def unused(b, n):
                if n == 0:
                    if not (isinstance(b, int) and b == 0):
                        act.wait_ge(moments_ready, MOMENTS * b)
                elif n <= QUANTA:
                    act.wait_ge(shift_sums, QUANTA * b + n)
                else:
                    act.wait_ge(moments_ready, MOMENTS * b + n - QUANTA)
                return junk[:]

            def quarter(slot, c, p):
                return xs[:, slot, c, 1 + HALF_ROWS // 2 * p:1 + HALF_ROWS // 2 * (p + 1), :].rearrange(
                    "p h w -> p (h w)")

            def bottom_sum(b, par, loads, c, p):
                if p == 0:
                    act.wait_ge(x_loaded[1 + par][c], 16 * loads)
                nc.scalar.activation(unused(b, 2 * c + p), quarter(1 + par, c, p), ACT.Identity,
                                     accum_out=sums[:, c, p:p + 1]).then_inc(shift_sums, 1)

            def bottom_square(b, par, c, p):
                nc.scalar.activation(unused(b, 4 + 2 * c + p), quarter(1 + par, c, p), ACT.Square,
                                     bias=neg_shift[:, c:c + 1],
                                     accum_out=squares[:, c, p:p + 1]).then_inc(moments_ready, 1)

            def top_sum(b, c, p):
                if p == 0:
                    act.wait_ge(x_loaded[0][c], 16 * (b + 1))
                nc.scalar.activation(unused(b, 8 + 2 * c + p), quarter(0, c, p), ACT.Identity,
                                     accum_out=sums[:, c, 2 + p:3 + p]).then_inc(moments_ready, 1)

            def top_square(b, c, p):
                nc.scalar.activation(unused(b, 12 + 2 * c + p), quarter(0, c, p), ACT.Square,
                                     bias=neg_shift[:, c:c + 1],
                                     accum_out=squares[:, c, 2 + p:3 + p]).then_inc(moments_ready, 1)

            def centre(slot, c, p):
                r0 = (1 if slot == 0 else 0) + 21 * p
                part = xs[:, slot, c, r0:r0 + 21 - p, :]
                nc.scalar.activation(part, part, ACT.Identity, bias=neg_mean[:, c:c + 1]
                                     ).then_inc(centred, 1)

            def take_root(b):
                act.wait_ge(var_ready, b + 1)
                nc.scalar.activation(std[:], var[:], ACT.Sqrt).then_inc(std_ready, 1)

            def round_hi(i, s, c):
                act.wait_ge(t_ready, NC * pair_no(i, s) + c + 1)
                nc.scalar.activation(stacked(u[:, s % U_SLOTS, c, 0, :, :, 1:W + 1]), stacked(t_rows[:, c]), ACT.Identity,
                                     scale=row_scale[:, s // IMG_PAIRS % 2, c:c + 1]).then_inc(hi_ready, 1)

            def evacuate(i, s, k):
                par, pair, j = s // IMG_PAIRS % 2, s % NP, PAIRS[s % NP][k]
                dest = {1: 0, 2: 1, 3: 3, 4: 4, 0: 3, 5: 5}[j]
                bias_at = {1: 0, 2: 1, 0: 2, 5: 3}.get(j)
                first = at_start(i, s, NP)
                half = half_no(i, s)
                for co in range(NC):
                    if co == 0:
                        if pair == 0 and not first:
                            act.wait_ge(mix_ready, MIX * half - (3 if k == 0 else 0))
                        if pair == 1 and k == 0 and not first:
                            act.wait_ge(y_done, FINALS * half)
                        if pair == 2:
                            act.wait_ge(y_done, FINALS * half + 4 - 2 * k)
                    act.wait_ge(pe_done, PRODS * pair_no(i, s) + NC * k + co + 1)
                    src = ps[:, 4 * k + 2 * co:4 * k + 2 * co + 2, 0:BANK]
                    dst = prod[:, co, dest, :].rearrange("p (g n) -> p g n", g=NG)
                    if bias_at is None:
                        nc.scalar.activation(dst, src, ACT.Identity, scale=evac_scale[:, j:j + 1]
                                             ).then_inc(prod_ready, 1)
                    else:
                        nc.scalar.activation(dst, src, ACT.Identity, scale=evac_scale[:, j:j + 1],
                                             bias=bias[:, par, bias_at, co:co + 1]
                                             ).then_inc(prod_ready, 1)

            def step(i, s, rounds, stats):
                q, par = s % IMG_PAIRS, s // IMG_PAIRS % 2
                b = 2 * i + s // IMG_PAIRS
                quarters = [(c, p) for c in range(NC) for p in range(2)]
                extra = []
                if q == 0:
                    extra = [lambda c=c, p=p: centre(1 + par, c, p) for c, p in quarters]
                if stats and q == 1:
                    extra = [lambda c=c, p=p: bottom_sum(b + 1, 1 - par, i + 1 + par, c, p) for c, p in quarters]
                if stats and q == 3:
                    act.wait_ge(shift_ready, b + 2)
                    extra = [lambda c=c, p=p: bottom_square(b + 1, 1 - par, c, p) for c, p in quarters]
                if stats and q == 4:
                    extra = [lambda c=c, p=p: top_sum(b + 1, c, p) for c, p in quarters]
                    extra += [lambda c=c, p=p: top_square(b + 1, c, p) for c, p in quarters]
                if not at_start(i, s, 1):
                    evacuate(i, s - 1, 1)
                if stats and q == 5:
                    take_root(b + 1)
                    act.wait_ge(mean_ready, b + 2)
                    for c, p in quarters:
                        centre(0, c, p)
                    act.wait_ge(norm_ready, b + 2)
                for c in range(NC):
                    if rounds:
                        round_hi(i, s + 1, c)
                    for _ in range(2):
                        if extra:
                            extra.pop(0)()
                evacuate(i, s, 0)
                while extra:
                    extra.pop(0)()

            quarters = [(c, p) for c in range(NC) for p in range(2)]

            def round_w(n):
                c, j = W_ORDER[n]
                if n < TRANSFORMED:
                    act.wait_ge(g_ready, n + 1)
                nc.scalar.activation(w_hi[:, c, j, :, :].rearrange("p t n -> p (t n)"), g_tile(n),
                                     ACT.Identity, scale=w_scale[:]).then_inc(whi_ready, 1)

            for c, p in quarters:
                bottom_sum(0, 0, 1, c, p)
            act.wait_ge(shift_ready, 1)
            for c, p in quarters:
                bottom_square(0, 0, c, p)
            for c, p in quarters:
                top_sum(0, c, p)
            act.wait_ge(scale_ready, 1)
            for n in range(4):
                round_w(n)
            for c, p in quarters:
                top_square(0, c, p)
            take_root(0)
            act.wait_ge(mean_ready, 1)
            for c, p in quarters:
                centre(0, c, p)
            act.wait_ge(norm_ready, 1)
            for c in range(NC):
                round_hi(0, 0, c)
            for n in range(4, len(W_ORDER)):
                round_w(n)
            step(0, 0, True, True)
            with act.Fori(0, NB // 2 - 1) as i:
                for s in range(1, 13):
                    step(i, s, True, True)
            for s in range(1, 12):
                step(NB // 2 - 1, s, s < 11, s < IMG_PAIRS)
            evacuate(NB // 2 - 1, 2 * IMG_PAIRS - 1, 1)

        @block.vector
        def _(dve):
            steps = [0]

            def small_step(ins):
                steps[0] += 1
                ins.then_inc(stat_step, 1)

            def settle(b):
                dve.wait_ge(stat_step, STEPS * b + steps[0])

            def group_sums(b):
                settle(b)
                small_step(nc.vector.transpose(turned[:], turn_in[:]))
                settle(b)
                small_step(nc.vector.tensor_reduce(grouped[:], turned[:].rearrange("p (g n) -> p g n", n=GROUP),
                                                   AX_X, ALU.add))
                settle(b)
                small_step(nc.vector.tensor_copy(spread[:].rearrange("p (g n) -> p g n", n=GROUP),
                                                 grouped[:, :, None].to_broadcast([P, 4, GROUP])))
                settle(b)
                small_step(nc.vector.transpose(turn_out[:], spread[:]))
                settle(b)

            def shift(b):
                steps[0] = 0
                dve.wait_ge(shift_sums, QUANTA * (b + 1))
                small_step(nc.vector.tensor_tensor(turn_in[:, 0:NC], sums[:, :, 0], sums[:, :, 1], ALU.add))
                group_sums(b)
                nc.vector.tensor_scalar(neg_shift[:], turn_out[:, 0:NC], -1.0 / (GROUP * HALF_ROWS * W), None,
                                        ALU.mult).then_inc(shift_ready, 1)

            def statistics(b, par):
                count = GROUP * H * W
                dve.wait_ge(moments_ready, MOMENTS * (b + 1))
                small_step(nc.vector.tensor_reduce(turn_in[:, 0:NC], sums[:], AX_X, ALU.add))
                small_step(nc.vector.tensor_reduce(turn_in[:, NC:2 * NC], squares[:], AX_X, ALU.add))
                group_sums(b)
                sum_x, sum_square = turn_out[:, 0:NC], turn_out[:, NC:2 * NC]
                nc.vector.tensor_scalar(neg_mean[:], sum_x, -1.0 / count, None, ALU.mult).then_inc(mean_ready, 1)
                small_step(nc.vector.scalar_tensor_tensor(out=small[:, 0, :], in0=sum_x, scalar=1.0 / count,
                                                          in1=neg_shift[:], op0=ALU.mult, op1=ALU.add))
                settle(b)
                small_step(nc.vector.tensor_tensor(small[:, 1, :], small[:, 0, :], small[:, 0, :], ALU.mult))
                settle(b)
                small_step(nc.vector.scalar_tensor_tensor(out=small[:, 2, :], in0=sum_square, scalar=1.0 / count,
                                                          in1=small[:, 1, :], op0=ALU.mult, op1=ALU.subtract))
                settle(b)
                nc.vector.tensor_scalar(var[:], small[:, 2, :], 0.0, EPS, ALU.max, ALU.add).then_inc(var_ready, 1)
                for n, share in enumerate(((1 / A2 + 1 / PA) / 2, (1 / A2 - 1 / PA) / 2, 1 - 1 / A2, 1 - A2)):
                    small_step(nc.vector.tensor_scalar(bias[:, par, n, :], sum_x, share / count, None, ALU.mult))
                dve.wait_ge(std_ready, b + 1)
                small_step(nc.vector.reciprocal(small[:, 3, :], std[:]))
                settle(b)
                small_step(nc.vector.tensor_tensor(small[:, 4, :], small[:, 3, :], small[:, 3, :], ALU.mult))
                settle(b)
                small_step(nc.vector.tensor_tensor(small[:, 5, :], small[:, 4, :], var[:], ALU.mult))
                settle(b)
                small_step(nc.vector.tensor_scalar(small[:, 6, :], small[:, 5, :], -0.5 * X_SCALE,
                                                   1.5 * X_SCALE, ALU.mult, ALU.add))
                settle(b)
                nc.vector.tensor_tensor(row_scale[:, par, :], small[:, 3, :], small[:, 6, :], ALU.mult
                                        ).then_inc(norm_ready, 1)
                assert steps[0] == STEPS, steps[0]

            def base(i, s, c):
                slot, pair = slot_of(s), s % NP
                if c == 0 and at_start(i, s, 1):
                    dve.wait_ge(pads_zero, 4)
                if pair == 0:
                    dve.wait_ge(centred, QUANTA * half_no(i, s) + 2 * c + 2)
                if not at_start(i, s, 1):
                    dve.wait_ge(t_ready, NC * (pair_no(i, s) - 1) + c + 1)
                near, far, scalar = ((1, 3, -B2), (1, 3, -A2), (2, 4, -(A2 + B2)))[pair]
                nc.vector.scalar_tensor_tensor(out=common[:, c].rearrange("p t k w -> p t (k w)"),
                                               in0=two_rows(slot, c, near), scalar=scalar,
                                               in1=two_rows(slot, c, far), op0=ALU.mult, op1=ALU.add
                                               ).then_inc(base_ready, 1)

            def transform(i, s, c):
                slot, pair = slot_of(s), s % NP
                dve.wait_ge(base_ready, NC * pair_no(i, s) + c + 1)
                if not at_start(i, s, 1):
                    dve.wait_ge(lo_ready, NC * (pair_no(i, s) - 1) + c + 1)
                if pair < 2:
                    for k in range(2):
                        ins = nc.vector.scalar_tensor_tensor(
                            out=t_rows[:, c, :, k, :], in0=common[:, c, :, 0, :],
                            scalar=(PA, PB)[pair] * (1 - 2 * k), in1=common[:, c, :, 1, :],
                            op0=ALU.mult, op1=ALU.add)
                else:
                    ins = nc.vector.scalar_tensor_tensor(
                        out=t_rows[:, c].rearrange("p t k w -> p t (k w)"), in0=two_rows(slot, c, 0),
                        scalar=A2 * B2, in1=common[:, c].rearrange("p t k w -> p t (k w)"),
                        op0=ALU.mult, op1=ALU.add)
                ins.then_inc(t_ready, 1)

            def round_lo(i, s, c):
                dve.wait_ge(hi_ready, NC * pair_no(i, s) + c + 1)
                nc.vector.scalar_tensor_tensor(out=stacked(u[:, s % U_SLOTS, c, 1, :, :, 1:W + 1]),
                                               in0=stacked(t_rows[:, c]),
                                               scalar=row_scale[:, s // IMG_PAIRS % 2, c:c + 1],
                                               in1=stacked(u[:, s % U_SLOTS, c, 0, :, :, 1:W + 1]),
                                               op0=ALU.mult, op1=ALU.subtract).then_inc(lo_ready, 1)

            def transform_pair(i, s):
                for c in range(NC):
                    base(i, s, c)
                for c in range(NC):
                    transform(i, s, c)
                for c in range(NC):
                    round_lo(i, s, c)

            def combine(i, s):
                slot, pair, half = slot_of(s), s % NP, half_no(i, s)
                M = [prod[:, :, k, :] for k in range(6)]

                def mixed(n):
                    dve.wait_ge(mix_ready, MIX * half + n)

                def add(out, in0, in1, op=ALU.add):
                    nc.vector.tensor_tensor(out, in0, in1, op).then_inc(mix_ready, 1)

                def add_scaled(out, in0, scalar, in1):
                    nc.vector.scalar_tensor_tensor(out=out, in0=in0, scalar=scalar, in1=in1, op0=ALU.mult,
                                                   op1=ALU.add).then_inc(mix_ready, 1)

                def finish(row, k):
                    y = rows(slot, slice(0, NC), 1 + row)
                    nc.vector.tensor_tensor(y, M[k].rearrange("p c (t w) -> p c t w", w=W), y, ALU.add
                                            ).then_inc(y_done, 1)

                def finish_scaled(row, k, scalar):
                    for co in range(NC):
                        y = rows(slot, co, 1 + row)
                        nc.vector.scalar_tensor_tensor(out=y, in0=plane(prod[:, co, k, :]), scalar=scalar, in1=y,
                                                       op0=ALU.mult, op1=ALU.add).then_inc(y_done, 1)

                if pair == 0:
                    dve.wait_ge(prod_ready, PRODS * (pair_no(i, s) + 1))
                    if not at_start(i, s, NP):
                        mixed(0)
                        dve.wait_ge(y_done, FINALS * half)
                    add(M[2], M[0], M[1])
                    mixed(1)
                    add(M[1], M[0], M[1], ALU.subtract)
                if pair == 1:
                    dve.wait_ge(prod_ready, PRODS * (pair_no(i, s) + 1))
                    mixed(2)
                    add(M[0], M[3], M[4])
                    mixed(3)
                    add(M[4], M[3], M[4], ALU.subtract)
                    add_scaled(M[5], M[0], (PB / PA) ** 2, M[2])
                    mixed(4)
                    add_scaled(M[3], M[4], PB / PA, M[1])
                    dve.wait_ge(t_ready, NC * NP * (half + 1))
                    mixed(5)
                    finish_scaled(2, 5, A2)
                    mixed(6)
                    finish_scaled(1, 3, PA)
                if pair == 2:
                    add(M[2], M[0], M[2])
                    add_scaled(M[1], M[4], (PB / PA) ** 3, M[1])
                    dve.wait_ge(prod_ready, PRODS * pair_no(i, s) + NC)
                    mixed(7)
                    add(M[3], M[2], M[3])
                    mixed(9)
                    finish(0, 3)
                    dve.wait_ge(prod_ready, PRODS * (pair_no(i, s) + 1))
                    add_scaled(M[5], M[1], PA ** 3, M[5])
                    mixed(10)
                    finish(3, 5)

            def step(i, s, more, stats):
                q, par, b = s % IMG_PAIRS, s // IMG_PAIRS % 2, 2 * i + s // IMG_PAIRS
                if stats and q == 5:
                    statistics(b + 1, 1 - par)
                if not at_start(i, s, 1):
                    combine(i, s - 1)
                if stats and q == 2:
                    shift(b + 1)
                if more:
                    transform_pair(i, s + 1)

            for n in range(2 * 5):
                c, m = n // 5, n % 5
                if m == 0:
                    dve.wait_ge(w_loaded[c], 16)
                dve.wait_ge(delta_ready, n + 1)
                part = w_full[:, c, 2 * m:min(2 * m + 2, 9), :].rearrange("p t n -> p (t n)")
                nc.vector.scalar_tensor_tensor(out=part, in0=ps[:, n % 8, 0:part.shape[1]], scalar=LORA_SCALE,
                                               in1=part, op0=ALU.mult, op1=ALU.add).then_inc(merged, 1)
                if m == 4:
                    dve.wait_ge(merged, n + 1)
                    for e, end in enumerate((ALU.max, ALU.min)):
                        nc.vector.tensor_reduce(w_ends[:, 2 * c + e:2 * c + e + 1],
                                                w_full[:, c].rearrange("p t n -> p (t n)"), AX_X, end
                                                ).then_inc(max_ready, 1)
            dve.wait_ge(turn_zero, 1)
            shift(0)
            dve.wait_ge(max_all, 1)
            nc.vector.tensor_reduce(w_max[:], w_ends_all[:], AX_X, ALU.max).then_inc(scale_step, 1)
            dve.wait_ge(scale_step, 1)
            nc.vector.tensor_scalar(w_floor[:], w_max[:], 1e-30, None, ALU.max).then_inc(scale_step, 1)
            dve.wait_ge(scale_step, 2)
            nc.vector.tensor_scalar(w_power[:].bitcast(U32), w_floor[:].bitcast(U32), 0x7F800000, None,
                                    ALU.bitwise_and).then_inc(scale_step, 1)
            dve.wait_ge(scale_step, 3)
            nc.vector.reciprocal(w_inverse[:], w_power[:]).then_inc(scale_step, 1)
            for j in range(NJ):
                nc.vector.tensor_scalar(evac_scale[:, j:j + 1], w_power[:],
                                        1.0 / (W_SCALE * X_SCALE * POINT_NORM[j]), None, ALU.mult
                                        ).then_inc(scale_step, 1)
            dve.wait_ge(scale_step, 4)
            nc.vector.tensor_scalar(w_scale[:], w_inverse[:], W_SCALE, None, ALU.mult
                                    ).then_inc(scale_ready, 1)

            def lo_w(n):
                c, j = W_ORDER[n]
                dve.wait_ge(whi_ready, n + 1)
                hi = w_hi[:, c, j, :, :].rearrange("p t n -> p (t n)")
                nc.vector.scalar_tensor_tensor(out=w_lo[:, c, j, :, :].rearrange("p t n -> p (t n)"), in0=g_tile(n),
                                               scalar=w_scale[:], in1=hi, op0=ALU.mult,
                                               op1=ALU.subtract).then_inc(wlo_ready, 1)

            def make_filters(m):
                c, p = m % 2, (PA, PB)[m // 2]
                even = prod[:, m % 2, 2, 0:TAPS * CH]
                if m >= 2:
                    dve.wait_ge(g_ready, 2 * m - 2)
                    dve.wait_ge(wlo_ready, 2 * m - 2)
                nc.vector.scalar_tensor_tensor(out=even, in0=g_row(c, 2), scalar=p * p, in1=g_row(c, 0),
                                               op0=ALU.mult, op1=ALU.add).then_inc(gbase_ready, 1)
                dve.wait_ge(gbase_ready, m + 1)
                for k in range(2):
                    nc.vector.scalar_tensor_tensor(out=g_tile(2 * m + k), in0=g_row(c, 1),
                                                   scalar=p * (1 - 2 * k), in1=even,
                                                   op0=ALU.mult, op1=ALU.add).then_inc(g_ready, 1)

            dve.wait_ge(scale_ready, 1)
            for m in (0, 1):
                make_filters(m)
            for n in range(4):
                lo_w(n)
            statistics(0, 0)
            transform_pair(0, 0)
            for m in (2, 3):
                make_filters(m)
            for n in range(4, len(W_ORDER)):
                lo_w(n)
            step(0, 0, True, True)
            dve.wait_ge(last_pad_zero, 1)
            with dve.Fori(0, NB // 2 - 1) as i:
                for s in range(1, 13):
                    step(i, s, True, True)
            for s in range(1, 13):
                step(NB // 2 - 1, s, s < 11, s < IMG_PAIRS)

        @block.tensor
        def _(pe):
            pe.wait_ge(lora_loaded, 32)
            for n in range(10):
                c, m = n // 5, n % 5
                if n >= 8:
                    pe.wait_ge(merged, n - 7)
                for tap in range(2 * m, min(2 * m + 2, 9)):
                    mm = nc.tensor.matmul(ps[:, n % 8, (tap % 2) * CH:(tap % 2 + 1) * CH],
                                          lora_a[:, tap, c * P:(c + 1) * P], lora_b, start=True, stop=True)
                mm.then_inc(delta_ready, 1)

            pe.wait_ge(pads_zero, 4)

            def multiply(Q, s):
                if isinstance(Q, int) and Q < NP:
                    pe.wait_ge(wlo_ready, 4 * (Q + 1))
                pe.wait_ge(lo_ready, NC * (Q + 1))
                for k in range(2):
                    for co in range(NC):
                        if not (isinstance(Q, int) and Q == 0):
                            pe.wait_ge(prod_ready, PRODS * (Q - 1) + NC * k + co + 1)
                        terms = [(w, hl, ci, kw) for w, hl in ((w_hi, 0), (w_lo, 0), (w_hi, 1))
                                 for ci in range(NC) for kw in range(TAPS)]
                        for n, (w, hl, ci, kw) in enumerate(terms):
                            for g in range(NG):
                                mm = nc.tensor.matmul(
                                    plane(ps[:, 4 * k + 2 * co + g, 0:BANK]),
                                    w[:, ci, PAIRS[s % NP][k], kw, co * P:(co + 1) * P],
                                    u[:, s % U_SLOTS, ci, hl, g * BANK_TILES:(g + 1) * BANK_TILES, k, kw:kw + W],
                                    start=(n == 0), stop=(n == len(terms) - 1))
                        mm.then_inc(pe_done, 1)

            for s in range(IMG_PAIRS):
                multiply(s, s)
            with pe.Fori(1, NB) as b:
                for s in range(IMG_PAIRS):
                    multiply(IMG_PAIRS * b + s, s)


def kernel(x, L0_conv_W0, L0_conv_lora_A, L0_conv_lora_B):
    import numpy as np
    import concourse.bacc as bacc
    from concourse import mybir as mb
    from concourse.bass_utils import run_bass_kernel_spmd

    x = np.ascontiguousarray(x)
    w0t = np.ascontiguousarray(np.asarray(L0_conv_W0).transpose(1, 2, 3, 0).reshape(CH, 9, CH))
    lora_at = np.ascontiguousarray(np.asarray(L0_conv_lora_A).reshape(RANK, CH, 9).transpose(0, 2, 1))
    lora_bt = np.ascontiguousarray(np.asarray(L0_conv_lora_B).T)
    arrays = {"x_dram": x, "w0t_dram": w0t, "lora_at_dram": lora_at, "lora_bt_dram": lora_bt}
    nc = bacc.Bacc("TRN2", target_bir_lowering=False, num_devices=1)
    args = [nc.dram_tensor(name, a.shape, mb.dt.from_np(a.dtype), kind="ExternalInput").ap()
            for name, a in arrays.items()]
    out = nc.dram_tensor("out_dram", x.shape, mb.dt.from_np(x.dtype), kind="ExternalOutput").ap()
    build(nc, *args, out)
    r = run_bass_kernel_spmd(nc, [arrays], core_ids=[0])
    return r.results[0]["out_dram"]
```

```python
from contextlib import ExitStack

import concourse.bass as bass
from concourse import mybir

ALU = mybir.AluOpType
ACT = mybir.ActivationFunctionType
AX_X = mybir.AxisListType.X
F32 = mybir.dt.float32
F16 = mybir.dt.float16
BF16 = mybir.dt.bfloat16
U32 = mybir.dt.uint32

P = 128
NB, CH, H, W = 8, 256, 80, 80
NC = CH // P
TAPS = 3
W_BANKS = (TAPS * TAPS + 1) // 2
TILE_ROWS = 4
NJ = TILE_ROWS + TAPS - 1
HALF_ROWS = H // 2
HALF_TILES = HALF_ROWS // TILE_ROWS
SLOT_ROWS = HALF_ROWS + 2
BANK_TILES = 5
NG = HALF_TILES // BANK_TILES
BANK = BANK_TILES * W
PLANE = HALF_TILES * W
RANK = 8
LORA_SCALE = 2.0
GROUP = 8
EPS = 1e-5

PA, PB = 0.75, 1.5
A2, B2 = PA * PA, PB * PB
POINT_NORM = [A2 * B2] + [2 * A2 * (A2 - B2)] * 2 + [2 * B2 * (B2 - A2)] * 2 + [1.0]
PAIRS = [(1, 2), (3, 4), (0, 5)]
NP = len(PAIRS)
IMG_PAIRS = 2 * NP
U_SLOTS = 2

X_SCALE = 32.0
W_SCALE = 4096.0

W_ORDER = [(c, j) for pair in PAIRS for c in range(NC) for j in pair]
TRANSFORMED = 2 * 2 * NC

PRODS = 2 * NC
MIX = 9
FINALS = 8
QUANTA = 4
MOMENTS = 3 * QUANTA
STEPS = 22
FIRST_STEPS = 13
STAT_COLS = BANK
STAT_PIECES = HALF_ROWS * W // STAT_COLS


def build(nc, x, w0t, lora_at, lora_bt, out):
    x_v = x.rearrange("b (c p) h w -> b c p (h w)", p=P)
    out_v = out.rearrange("b (c p) h w -> b c p (h w)", p=P)

    with ExitStack() as ctx:
        def sb(name, shape, dt):
            return ctx.enter_context(nc.sbuf_tensor(name, shape, dt))

        def sem(name):
            return ctx.enter_context(nc.semaphore(name))

        xs = sb("xs", [P, 3, NC, SLOT_ROWS, W], F32)
        w_hi = sb("w_hi", [P, NC, NJ, TAPS, CH], F16)
        w_lo = sb("w_lo", [P, NC, NJ, TAPS, CH], F16)
        u = sb("u", [P, U_SLOTS, NC, 2, HALF_TILES, 2, W + 2], F16)
        common = sb("common", [P, NC, HALF_TILES, 2, W], F32)
        t_rows = sb("t_rows", [P, NC, HALF_TILES, 2, W], F32)
        prod = sb("prod", [P, NC, 6, PLANE], F32)
        junk = sb("junk", [P, HALF_ROWS // 2 * W], BF16)
        evac_scale = sb("evac_scale", [P, NJ], F32)
        w_end = sb("w_end", [P, 1], F32)
        w_max = sb("w_max", [P, 1], F32)
        w_floor = sb("w_floor", [P, 1], F32)
        w_power = sb("w_power", [P, 1], F32)
        w_inverse = sb("w_inverse", [P, 1], F32)
        w_scale = sb("w_scale", [P, 1], F32)
        sums = sb("sums", [P, NC, 2 * 2], F32)
        squares = sb("squares", [P, NC, 2 * 2], F32)
        first_stats = sb("first_stats", [P, 2 * STAT_PIECES, 6], F32)
        first_moments = sb("first_moments", [P, 2], F32)
        first_offset = sb("first_offset", [P, 2], F32)
        neg_shift = sb("neg_shift", [P, NC], F32)
        neg_mean = sb("neg_mean", [P, NC], F32)
        var = sb("var", [P, NC], F32)
        std = sb("std", [P, NC], F32)
        small = sb("small", [P, 7, NC], F32)
        turn_in = sb("turn_in", [P, 32], F32)
        turned = sb("turned", [P, 32], F32)
        grouped = sb("grouped", [P, 4], F32)
        spread = sb("spread", [P, 32], F32)
        turn_out = sb("turn_out", [P, 32], F32)
        row_scale = sb("row_scale", [P, 2, NC], F32)
        bias = sb("bias", [P, 2, 4, NC], F32)
        ps = ctx.enter_context(nc.psum_tensor("ps", [P, 8, 512], F32))
        w_full = xs[:, 2].rearrange("p c h w -> p (c h w)")[:, 0:NC * 9 * CH].rearrange(
            "p (c t n) -> p c t n", c=NC, t=9)
        lora = t_rows[0:RANK].rearrange("r c t k w -> r (c t k w)")
        lora_a = lora[:, 0:9 * CH].rearrange("r (t n) -> r t n", t=9)
        lora_b = lora[:, 9 * CH:10 * CH]

        magnitude = w_lo[:].rearrange("p c (k j) t n -> p c k (j t n)", k=2).bitcast(BF16)
        w_size = [magnitude[:, c, 0, :] for c in range(NC)]
        w_sizes = magnitude[:, 0, 1, :]
        w_sizes_half = magnitude[:, 1, 1, 0:9 * CH // 2]

        w_loaded = [sem(f"w_loaded{c}") for c in range(NC)]
        lora_loaded = sem("lora_loaded")
        x_loaded = [[sem(f"x_loaded{s}{c}") for c in range(NC)] for s in range(3)]
        stored = [[sem(f"stored{s}{c}") for c in range(NC)] for s in range(3)]
        pads_zero = sem("pads_zero")
        last_pad_zero = sem("last_pad_zero")
        stats_zero = sem("stats_zero")
        delta_ready = sem("delta_ready")
        merged = sem("merged")
        sizes_ready = sem("sizes_ready")
        max_step = sem("max_step")
        max_ready = sem("max_ready")
        max_all = sem("max_all")
        scale_step = sem("scale_step")
        scale_ready = sem("scale_ready")
        evac_ready = sem("evac_ready")
        gbase_ready = sem("gbase_ready")
        g_ready = sem("g_ready")
        whi_ready = sem("whi_ready")
        wlo_ready = sem("wlo_ready")
        shift_sums = sem("shift_sums")
        first_pieces = sem("first_pieces")
        shift_ready = sem("shift_ready")
        moments_ready = sem("moments_ready")
        stat_step = sem("stat_step")
        mean_ready = sem("mean_ready")
        var_ready = sem("var_ready")
        std_ready = sem("std_ready")
        norm_ready = sem("norm_ready")
        centred = sem("centred")
        base_ready = sem("base_ready")
        t_ready = sem("t_ready")
        hi_ready = sem("hi_ready")
        lo_ready = sem("lo_ready")
        pe_done = sem("pe_done")
        prod_ready = sem("prod_ready")
        mix_ready = sem("mix_ready")
        y_done = sem("y_done")

        def rows(slot, c, k):
            return xs[:, slot, c, k:k + TILE_ROWS * (HALF_TILES - 1) + 1:TILE_ROWS, :]

        def two_rows(slot, c, k):
            start = 0 if k < 2 else 2
            tiles = xs[:, slot, c, start:start + HALF_ROWS, :].rearrange("p (t r) w -> p t r w", r=TILE_ROWS)
            return tiles[:, :, k - start:k - start + 2, :].rearrange("p t r w -> p t (r w)")

        def stacked(ap):
            return ap.rearrange("p t k w -> p (t k) w")

        def pair_no(i, s):
            return 2 * IMG_PAIRS * i + s

        def half_no(i, s):
            return 4 * i + s // NP

        def at_start(i, s, n):
            return isinstance(i, int) and pair_no(i, s) < n

        def slot_of(s):
            return 0 if s // NP % 2 == 0 else 1 + s // IMG_PAIRS % 2

        def plane(ap):
            return ap.rearrange("p (t w) -> p t w", w=W)

        def g_row(c, kh):
            return w_full[:, c, 3 * kh:3 * kh + 3, :].rearrange("p t n -> p (t n)")

        def g_tile(n):
            c, j = W_ORDER[n]
            if n >= TRANSFORMED:
                return g_row(c, 0 if j == 0 else TAPS - 1)
            return prod[:, c, 3 * (n // 4) + n % 2, 0:TAPS * CH]

        block = ctx.enter_context(nc.Block())

        @block.sync
        def _(sp):
            def load_top(b, c):
                sp.dma_start(xs[:, 0, c, 1:SLOT_ROWS, :].rearrange("p h w -> p (h w)"),
                             x_v[b, c, :, 0:(HALF_ROWS + 1) * W]).then_inc(x_loaded[0][c], 16)

            def load_bottom(b, par, c):
                sp.dma_start(xs[:, 1 + par, c, 0:SLOT_ROWS - 1, :].rearrange("p h w -> p (h w)"),
                             x_v[b, c, :, (HALF_ROWS - 1) * W:H * W]).then_inc(x_loaded[1 + par][c], 16)

            def store(b, slot, half, c):
                sp.dma_start(out_v[b, c, :, half * HALF_ROWS * W:(half + 1) * HALF_ROWS * W],
                             xs[:, slot, c, 1:HALF_ROWS + 1, :].rearrange("p h w -> p (h w)")
                             ).then_inc(stored[slot][c], 16)

            def images(i, last):
                for par in range(2):
                    b = 2 * i + par
                    more = not (last and par == 1)
                    if more:
                        for c in range(NC):
                            if not (isinstance(i, int) and i + par == 0):
                                sp.wait_ge(stored[2 - par][c], 16 * (i + par))
                            else:
                                sp.wait_ge(wlo_ready, NC * NJ)
                            load_bottom(b + 1, 1 - par, c)
                    sp.wait_ge(y_done, 2 * FINALS * b + FINALS)
                    for c in range(NC):
                        store(b, 0, 0, c)
                    if more:
                        for c in range(NC):
                            sp.wait_ge(stored[0][c], 16 * (b + 1))
                        for c in reversed(range(NC)):
                            load_top(b + 1, c)
                    if more:
                        sp.wait_ge(y_done, 2 * FINALS * b + 2 * FINALS)
                        for c in range(NC):
                            store(b, 1 + par, 1, c)

            sp.dma_start(lora_a, lora_at).then_inc(lora_loaded, 16)
            sp.dma_start(lora_b, lora_bt).then_inc(lora_loaded, 16)
            for c in range(NC):
                sp.dma_start(w_full[:, c], w0t[c * P:(c + 1) * P]).then_inc(w_loaded[c], 16)
            for c in reversed(range(NC)):
                load_bottom(0, 0, c)
            for c in reversed(range(NC)):
                load_top(0, c)
            images(0, False)
            with sp.Fori(1, NB // 2 - 1) as i:
                images(i, False)
            images(NB // 2 - 1, True)
            y_finished = 2 * FINALS * NB
            last_out = out_v[NB - 1, 1, :, HALF_ROWS * W:H * W].rearrange("p (t r w) -> p t (r w)", t=HALF_TILES,
                                                                          w=W)
            last_rows = xs[:, 2, 1, 1:HALF_ROWS + 1, :].rearrange("p (t r) w -> p t (r w)", r=TILE_ROWS)
            cut = (TILE_ROWS - 1) * W
            sp.wait_ge(y_done, y_finished - 1)
            sp.dma_start(last_out[:, :, 0:cut], last_rows[:, :, 0:cut]).then_inc(stored[2][1], 16)
            sp.wait_ge(y_done, y_finished)
            store(NB - 1, 2, 1, 0)
            sp.wait_ge(y_done, y_finished + 1)
            sp.dma_start(last_out[:, :, cut:], last_rows[:, :, cut:]).then_inc(stored[2][1], 16)
            for c in range(NC):
                sp.wait_ge(stored[0][c], 16 * NB)
                sp.wait_ge(stored[1][c], 16 * (NB // 2))
                sp.wait_ge(stored[2][c], 16 * (NB // 2 + c))

        @block.gpsimd
        def _(pool):
            def make_filters(m):
                c, p = m % 2, (PA, PB)[m // 2]
                even = prod[:, c, 3 * (m // 2) + 2, 0:TAPS * CH]
                pool.wait_ge(merged, W_BANKS * (c + 1))
                odd = g_tile(2 * m + 1)
                nc.gpsimd.tensor_scalar(even, g_row(c, 2), p * p, None, ALU.mult).then_inc(gbase_ready, 1)
                nc.gpsimd.tensor_scalar(odd, g_row(c, 1), p, None, ALU.mult).then_inc(gbase_ready, 1)
                pool.wait_ge(gbase_ready, 3 * m + 1)
                nc.gpsimd.tensor_tensor(even, even, g_row(c, 0), ALU.add).then_inc(gbase_ready, 1)
                if m == 1:
                    pool.wait_ge(max_ready, 1)
                    nc.gpsimd.partition_all_reduce(w_max[:], w_end[:], P,
                                                   bass.bass_isa.ReduceOp.absmax).then_inc(max_all, 1)
                pool.wait_ge(gbase_ready, 3 * m + 3)
                nc.gpsimd.tensor_tensor(g_tile(2 * m), even, odd, ALU.add).then_inc(g_ready, 1)
                pool.wait_ge(g_ready, 2 * m + 1)
                nc.gpsimd.tensor_tensor(odd, even, odd, ALU.subtract).then_inc(g_ready, 1)

            nc.gpsimd.memset(turn_in[:], 0.0).then_inc(stats_zero, 1)
            nc.gpsimd.memset(sums[:], 0.0).then_inc(stats_zero, 1)
            nc.gpsimd.memset(squares[:], 0.0).then_inc(stats_zero, 1)
            u_rows = u[:].rearrange("p s c l t k w -> p (s c l t k) w")
            nc.gpsimd.memset(u_rows[:, :, 0:1], 0.0).then_inc(pads_zero, 1)
            nc.gpsimd.memset(u_rows[:, :, W + 1:W + 2], 0.0).then_inc(pads_zero, 1)
            nc.gpsimd.memset(xs[:, 0, :, 0, :], 0.0).then_inc(pads_zero, 1)
            nc.gpsimd.memset(xs[:, 1, :, SLOT_ROWS - 1, :], 0.0).then_inc(pads_zero, 1)
            for m in range(4):
                make_filters(m)
            pool.wait_ge(wlo_ready, NC * NJ)
            nc.gpsimd.memset(xs[:, 2, :, SLOT_ROWS - 1, :], 0.0).then_inc(last_pad_zero, 1)

        @block.scalar
        def _(act):
            quarters = [(c, p) for c in range(NC) for p in range(2)]

            def unused(b, n):
                if n == 0:
                    if not (isinstance(b, int) and b == 0):
                        act.wait_ge(moments_ready, MOMENTS * b)
                elif n <= QUANTA:
                    act.wait_ge(shift_sums, QUANTA * b + n)
                else:
                    act.wait_ge(moments_ready, MOMENTS * b + n - QUANTA)
                return junk[:]

            pieces = [0]

            def next_piece(both):
                n = pieces[0]
                pieces[0] = (n + both) % (QUANTA + MOMENTS)
                return n

            def quarter(slot, c, p):
                return xs[:, slot, c, 1 + HALF_ROWS // 2 * p:1 + HALF_ROWS // 2 * (p + 1), :].rearrange(
                    "p h w -> p (h w)")

            def bottom_sum(b, par, loads, c, p, both=1):
                if p == 0:
                    act.wait_ge(x_loaded[1 + par][c], 16 * loads)
                nc.scalar.activation(unused(b, next_piece(both)), quarter(1 + par, c, p), ACT.Identity,
                                     accum_out=sums[:, c, p:p + 1]).then_inc(shift_sums, both)

            def bottom_square(b, par, c, p, both=1):
                nc.scalar.activation(unused(b, next_piece(both)), quarter(1 + par, c, p), ACT.Square,
                                     bias=neg_shift[:, c:c + 1],
                                     accum_out=squares[:, c, p:p + 1]).then_inc(moments_ready, both)

            def top_sum(b, c, p, both=1):
                if p == 0:
                    act.wait_ge(x_loaded[0][c], 16 * (b + 1))
                nc.scalar.activation(unused(b, next_piece(both)), quarter(0, c, p), ACT.Identity,
                                     accum_out=sums[:, c, 2 + p:3 + p]).then_inc(moments_ready, both)

            def top_square(b, c, p, both=1):
                nc.scalar.activation(unused(b, next_piece(both)), quarter(0, c, p), ACT.Square,
                                     bias=neg_shift[:, c:c + 1],
                                     accum_out=squares[:, c, 2 + p:3 + p]).then_inc(moments_ready, both)

            def top_moments(b, c, both=1):
                for p in range(2):
                    top_sum(b, c, p, both)
                for p in range(2):
                    top_square(b, c, p, both)

            def centre(slot, c, p):
                r0 = (1 if slot == 0 else 0) + 21 * p
                part = xs[:, slot, c, r0:r0 + 21 - p, :]
                nc.scalar.activation(part, part, ACT.Identity, bias=neg_mean[:, c:c + 1]
                                     ).then_inc(centred, 1)

            def take_root(b):
                act.wait_ge(var_ready, b + 1)
                nc.scalar.activation(std[:], var[:], ACT.Sqrt).then_inc(std_ready, 1)

            def round_hi(i, s, c):
                if c == 0 and not at_start(i, s, U_SLOTS):
                    act.wait_ge(pe_done, PRODS * (pair_no(i, s) - U_SLOTS + 1))
                act.wait_ge(t_ready, NC * pair_no(i, s) + c + 1)
                nc.scalar.activation(stacked(u[:, s % U_SLOTS, c, 0, :, :, 1:W + 1]), stacked(t_rows[:, c]),
                                     ACT.Identity, scale=row_scale[:, s // IMG_PAIRS % 2, c:c + 1]).then_inc(hi_ready, 1)

            def evacuate(i, s, k):
                par, pair, j = s // IMG_PAIRS % 2, s % NP, PAIRS[s % NP][k]
                dest = {1: 0, 2: 1, 3: 3, 4: 4, 0: 3, 5: 5}[j]
                bias_at = {1: 0, 2: 1, 0: 2, 5: 3}.get(j)
                first = at_start(i, s, NP)
                half = half_no(i, s)
                for co in range(NC):
                    if co == 0:
                        if pair == 0 and k == 0 and not first:
                            act.wait_ge(mix_ready, MIX * half - 2)
                        if pair == 0 and k == 1 and not first:
                            act.wait_ge(y_done, FINALS * half)
                        if pair == 1 and k == 0 and not first:
                            act.wait_ge(y_done, FINALS * half)
                        if pair == 2 and k == 0:
                            act.wait_ge(mix_ready, MIX * half + 4)
                        if pair == 2 and k == 1:
                            act.wait_ge(y_done, FINALS * half + 4)
                    act.wait_ge(pe_done, PRODS * pair_no(i, s) + NC * k + co + 1)
                    src = ps[:, 4 * k + 2 * co:4 * k + 2 * co + 2, 0:BANK]
                    dst = prod[:, co, dest, :].rearrange("p (g n) -> p g n", g=NG)
                    if bias_at is None:
                        nc.scalar.activation(dst, src, ACT.Identity, scale=evac_scale[:, j:j + 1]
                                             ).then_inc(prod_ready, 1)
                    else:
                        nc.scalar.activation(dst, src, ACT.Identity, scale=evac_scale[:, j:j + 1],
                                             bias=bias[:, par, bias_at, co:co + 1]
                                             ).then_inc(prod_ready, 1)

            def step(i, s, rounds, stats):
                q, par = s % IMG_PAIRS, s // IMG_PAIRS % 2
                b = 2 * i + s // IMG_PAIRS
                if stats and q == 5:
                    act.wait_ge(norm_ready, b + 2)
                if rounds and q != 3:
                    for c in range(NC):
                        round_hi(i, s + 1, c)
                if not at_start(i, s, 1):
                    evacuate(i, s - 1, 1)
                if rounds and q == 3:
                    for c in range(NC):
                        round_hi(i, s + 1, c)
                if q == 0:
                    for c, p in quarters:
                        centre(1 + par, c, p)
                if stats and q == 1:
                    for c, p in quarters:
                        bottom_sum(b + 1, 1 - par, i + 1 + par, c, p)
                if stats and q == 3:
                    act.wait_ge(shift_ready, b + 2)
                    for c, p in quarters:
                        bottom_square(b + 1, 1 - par, c, p)
                if stats and q == 4:
                    top_moments(b + 1, 1)
                evacuate(i, s, 0)
                if stats and q == 4:
                    top_moments(b + 1, 0)
                    take_root(b + 1)
                    act.wait_ge(mean_ready, b + 2)
                    for c, p in quarters:
                        centre(0, c, p)

            def round_w(n):
                c, j = W_ORDER[n]
                if n < TRANSFORMED:
                    act.wait_ge(g_ready, n + 1)
                nc.scalar.activation(w_hi[:, c, j, :, :].rearrange("p t n -> p (t n)"), g_tile(n),
                                     ACT.Identity, scale=w_scale[:]).then_inc(whi_ready, 1)

            def magnitudes(c):
                act.wait_ge(merged, W_BANKS * (c + 1))
                nc.scalar.activation(w_size[c], w_full[:, c].rearrange("p t n -> p (t n)"), ACT.Abs
                                     ).then_inc(sizes_ready, 1)

            magnitudes(0)
            act.wait_ge(stats_zero, 3)
            for p in range(2):
                bottom_sum(0, 0, 1, 1, p, both=2)
            act.wait_ge(shift_ready, 1)
            for p in range(2):
                bottom_square(0, 0, 1, p, both=2)
            magnitudes(1)
            top_moments(0, 1, both=2)
            act.wait_ge(scale_ready, 1)
            for n in range(4):
                round_w(n)
            take_root(0)
            act.wait_ge(mean_ready, 1)
            for c, p in quarters:
                centre(0, c, p)
            act.wait_ge(norm_ready, 1)
            for c in range(NC):
                round_hi(0, 0, c)
            for n in range(4, len(W_ORDER)):
                round_w(n)
            act.wait_ge(evac_ready, NJ)
            step(0, 0, True, True)
            for s in range(1, 2 * IMG_PAIRS + 1):
                step(0, s, True, True)
            with act.Fori(1, NB // 2 - 1) as i:
                for s in range(1, 2 * IMG_PAIRS + 1):
                    step(i, s, True, True)
            for s in range(1, 2 * IMG_PAIRS):
                step(NB // 2 - 1, s, s < 2 * IMG_PAIRS - 1, s < IMG_PAIRS)
            evacuate(NB // 2 - 1, 2 * IMG_PAIRS - 1, 1)

        @block.vector
        def _(dve):
            steps = [0]

            def small_step(ins):
                steps[0] += 1
                ins.then_inc(stat_step, 1)

            def settle(b):
                first = isinstance(b, int) and b == 0
                dve.wait_ge(stat_step, STEPS * b + steps[0] + (0 if first else FIRST_STEPS))

            def group_sums(b):
                settle(b)
                small_step(nc.vector.transpose(turned[:], turn_in[:]))
                settle(b)
                small_step(nc.vector.tensor_reduce(grouped[:], turned[:].rearrange("p (g n) -> p g n", n=GROUP),
                                                   AX_X, ALU.add))
                settle(b)
                small_step(nc.vector.tensor_copy(spread[:].rearrange("p (g n) -> p g n", n=GROUP),
                                                 grouped[:, :, None].to_broadcast([P, 4, GROUP])))
                settle(b)
                small_step(nc.vector.transpose(turn_out[:], spread[:]))
                settle(b)

            def shift(b):
                steps[0] = 0
                dve.wait_ge(shift_sums, QUANTA * (b + 1))
                small_step(nc.vector.tensor_tensor(turn_in[:, 0:NC], sums[:, :, 0], sums[:, :, 1], ALU.add))
                group_sums(b)
                nc.vector.tensor_scalar(neg_shift[:], turn_out[:, 0:NC], -1.0 / (GROUP * HALF_ROWS * W), None,
                                        ALU.mult).then_inc(shift_ready, 1)

            def statistics(b, par):
                count = GROUP * H * W
                dve.wait_ge(moments_ready, MOMENTS * (b + 1))
                small_step(nc.vector.tensor_reduce(turn_in[:, 0:NC], sums[:], AX_X, ALU.add))
                small_step(nc.vector.tensor_reduce(turn_in[:, NC:2 * NC], squares[:], AX_X, ALU.add))
                group_sums(b)
                sum_x, sum_square = turn_out[:, 0:NC], turn_out[:, NC:2 * NC]
                nc.vector.tensor_scalar(neg_mean[:], sum_x, -1.0 / count, None, ALU.mult).then_inc(mean_ready, 1)
                small_step(nc.vector.scalar_tensor_tensor(out=small[:, 0, :], in0=sum_x, scalar=1.0 / count,
                                                          in1=neg_shift[:], op0=ALU.mult, op1=ALU.add))
                settle(b)
                small_step(nc.vector.tensor_tensor(small[:, 1, :], small[:, 0, :], small[:, 0, :], ALU.mult))
                settle(b)
                small_step(nc.vector.scalar_tensor_tensor(out=small[:, 2, :], in0=sum_square, scalar=1.0 / count,
                                                          in1=small[:, 1, :], op0=ALU.mult, op1=ALU.subtract))
                settle(b)
                nc.vector.tensor_scalar(var[:], small[:, 2, :], 0.0, EPS, ALU.max, ALU.add).then_inc(var_ready, 1)
                for n, share in enumerate(((1 / A2 + 1 / PA) / 2, (1 / A2 - 1 / PA) / 2, 1 - 1 / A2, 1 - A2)):
                    small_step(nc.vector.tensor_scalar(bias[:, par, n, :], sum_x, share / count, None, ALU.mult))
                dve.wait_ge(std_ready, b + 1)
                small_step(nc.vector.reciprocal(small[:, 3, :], std[:]))
                settle(b)
                small_step(nc.vector.tensor_tensor(small[:, 4, :], small[:, 3, :], small[:, 3, :], ALU.mult))
                settle(b)
                small_step(nc.vector.tensor_tensor(small[:, 5, :], small[:, 4, :], var[:], ALU.mult))
                settle(b)
                small_step(nc.vector.tensor_scalar(small[:, 6, :], small[:, 5, :], -0.5 * X_SCALE,
                                                   1.5 * X_SCALE, ALU.mult, ALU.add))
                settle(b)
                nc.vector.tensor_tensor(row_scale[:, par, :], small[:, 3, :], small[:, 6, :], ALU.mult
                                        ).then_inc(norm_ready, 1)
                assert steps[0] == STEPS + (FIRST_STEPS if isinstance(b, int) and b == 0 else 0), steps[0]

            def base(i, s, c):
                slot, pair = slot_of(s), s % NP
                if c == 0 and at_start(i, s, 1):
                    dve.wait_ge(pads_zero, 4)
                if pair == 0:
                    dve.wait_ge(centred, QUANTA * half_no(i, s) + 2 * c + 2)
                if not at_start(i, s, 1):
                    dve.wait_ge(t_ready, NC * (pair_no(i, s) - 1) + c + 1)
                near, far, scalar = ((1, 3, -B2), (1, 3, -A2), (2, 4, -(A2 + B2)))[pair]
                nc.vector.scalar_tensor_tensor(out=common[:, c].rearrange("p t k w -> p t (k w)"),
                                               in0=two_rows(slot, c, near), scalar=scalar,
                                               in1=two_rows(slot, c, far), op0=ALU.mult, op1=ALU.add
                                               ).then_inc(base_ready, 1)

            def transform(i, s, c):
                slot, pair = slot_of(s), s % NP
                dve.wait_ge(base_ready, NC * pair_no(i, s) + c + 1)
                if not at_start(i, s, 1):
                    dve.wait_ge(lo_ready, NC * (pair_no(i, s) - 1) + c + 1)
                if pair < 2:
                    for k in range(2):
                        ins = nc.vector.scalar_tensor_tensor(
                            out=t_rows[:, c, :, k, :], in0=common[:, c, :, 0, :],
                            scalar=(PA, PB)[pair] * (1 - 2 * k), in1=common[:, c, :, 1, :],
                            op0=ALU.mult, op1=ALU.add)
                else:
                    ins = nc.vector.scalar_tensor_tensor(
                        out=t_rows[:, c].rearrange("p t k w -> p t (k w)"), in0=two_rows(slot, c, 0),
                        scalar=A2 * B2, in1=common[:, c].rearrange("p t k w -> p t (k w)"),
                        op0=ALU.mult, op1=ALU.add)
                ins.then_inc(t_ready, 1)

            def round_lo(i, s, c):
                dve.wait_ge(hi_ready, NC * pair_no(i, s) + c + 1)
                nc.vector.scalar_tensor_tensor(out=stacked(u[:, s % U_SLOTS, c, 1, :, :, 1:W + 1]),
                                               in0=stacked(t_rows[:, c]),
                                               scalar=row_scale[:, s // IMG_PAIRS % 2, c:c + 1],
                                               in1=stacked(u[:, s % U_SLOTS, c, 0, :, :, 1:W + 1]),
                                               op0=ALU.mult, op1=ALU.subtract).then_inc(lo_ready, 1)

            def transform_pair(i, s):
                for c in range(NC):
                    base(i, s, c)
                for c in range(NC):
                    transform(i, s, c)

            def round_pair(i, s):
                for c in range(NC):
                    round_lo(i, s, c)

            def combine(i, s, last=False):
                slot, pair, half = slot_of(s), s % NP, half_no(i, s)
                M = [prod[:, :, k, :] for k in range(6)]

                def mixed(n):
                    dve.wait_ge(mix_ready, MIX * half + n)

                def add(out, in0, in1, op=ALU.add):
                    nc.vector.tensor_tensor(out, in0, in1, op).then_inc(mix_ready, 1)

                def add_scaled(out, in0, scalar, in1):
                    nc.vector.scalar_tensor_tensor(out=out, in0=in0, scalar=scalar, in1=in1, op0=ALU.mult,
                                                   op1=ALU.add).then_inc(mix_ready, 1)

                def finish(row, k):
                    y = rows(slot, slice(0, NC), 1 + row)
                    nc.vector.tensor_tensor(y, M[k].rearrange("p c (t w) -> p c t w", w=W), y, ALU.add
                                            ).then_inc(y_done, 1)

                def finish_scaled(row, k, scalar):
                    for co in range(NC):
                        y = rows(slot, co, 1 + row)
                        nc.vector.scalar_tensor_tensor(out=y, in0=plane(prod[:, co, k, :]), scalar=scalar, in1=y,
                                                       op0=ALU.mult, op1=ALU.add).then_inc(y_done, 1)

                if pair == 0:
                    dve.wait_ge(prod_ready, PRODS * (pair_no(i, s) + 1))
                    if not at_start(i, s, NP):
                        mixed(0)
                        dve.wait_ge(y_done, FINALS * half)
                    add(M[2], M[0], M[1])
                    mixed(1)
                    add(M[1], M[0], M[1], ALU.subtract)
                if pair == 1:
                    dve.wait_ge(prod_ready, PRODS * (pair_no(i, s) + 1))
                    mixed(2)
                    add(M[0], M[3], M[4])
                    mixed(3)
                    add(M[4], M[3], M[4], ALU.subtract)
                    add_scaled(M[5], M[0], (PB / PA) ** 2, M[2])
                    mixed(4)
                    add_scaled(M[1], M[4], PB / PA, M[1])
                    dve.wait_ge(t_ready, NC * NP * (half + 1))
                    mixed(5)
                    finish_scaled(2, 5, A2)
                    mixed(6)
                    finish_scaled(1, 1, PA)
                if pair == 2:
                    add(M[2], M[0], M[2])
                    dve.wait_ge(y_done, FINALS * half + 4)
                    add_scaled(M[1], M[4], (PB / PA) ** 3 - PB / PA, M[1])
                    dve.wait_ge(prod_ready, PRODS * pair_no(i, s) + NC)
                    mixed(7)
                    add(M[3], M[2], M[3])
                    mixed(8)
                    finish_scaled(3, 1, PA ** 3)
                    mixed(9)
                    finish(0, 3)
                    dve.wait_ge(y_done, FINALS * half + 6)
                    if not last:
                        dve.wait_ge(prod_ready, PRODS * (pair_no(i, s) + 1))
                        finish(3, 5)
                    else:
                        for co in range(NC):
                            dve.wait_ge(prod_ready, PRODS * pair_no(i, s) + NC + co + 1)
                            y = rows(slot, co, 4)
                            nc.vector.tensor_tensor(y, plane(prod[:, co, 5, :]), y, ALU.add).then_inc(y_done, 1)

            def step(i, s, pairs, stats):
                q, par, b = s % IMG_PAIRS, s // IMG_PAIRS % 2, 2 * i + s // IMG_PAIRS
                if q != 3 and pairs > 1:
                    round_pair(i, s + 1)
                if not at_start(i, s, 1):
                    combine(i, s - 1, last=pairs == 0)
                if q == 3 and pairs > 1:
                    round_pair(i, s + 1)
                if stats and q == 2:
                    shift(b + 1)
                if stats and q == 4:
                    statistics(b + 1, 1 - par)
                if pairs > 2:
                    transform_pair(i, s + 2)

            def merge(n):
                c, m = n // W_BANKS, n % W_BANKS
                if m == 0:
                    dve.wait_ge(w_loaded[c], 16)
                dve.wait_ge(delta_ready, n + 1)
                part = w_full[:, c, 2 * m:min(2 * m + 2, 9), :].rearrange("p t n -> p (t n)")
                nc.vector.scalar_tensor_tensor(out=part, in0=ps[:, n % 8, 0:part.shape[1]], scalar=LORA_SCALE,
                                               in1=part, op0=ALU.mult, op1=ALU.add).then_inc(merged, 1)

            def channel_stats(slot, pieces):
                dve.wait_ge(x_loaded[slot][0], 16)
                half = xs[:, slot, 0, 1:HALF_ROWS + 1, :].rearrange("p h w -> p (h w)")
                for n in pieces:
                    at = (STAT_PIECES if slot == 0 else 0) + n
                    nc.vector.bn_stats(first_stats[:, at, :], half[:, n * STAT_COLS:(n + 1) * STAT_COLS]
                                       ).then_inc(first_pieces, 1)

            def channel_moments(halves):
                dve.wait_ge(first_pieces, STAT_PIECES * halves)
                small_step(nc.vector.bn_aggr(first_moments[:], first_stats[:, 0:STAT_PIECES * halves, :]
                                             .rearrange("p n k -> p (n k)")))
                settle(0)
                small_step(nc.vector.tensor_scalar(sums[:, 0, 0:1], first_moments[:, 0:1],
                                                   float(HALF_ROWS * W * halves), None, ALU.mult))

            def shift_chunk_0():
                channel_moments(1)
                settle(0)
                small_step(nc.vector.tensor_copy(turn_in[:, 0:1], sums[:, 0, 0:1]))
                group_sums(0)
                small_step(nc.vector.tensor_scalar(neg_shift[:, 0:1], turn_out[:, 0:1],
                                                   -1.0 / (GROUP * HALF_ROWS * W), None, ALU.mult))

            def squares_chunk_0():
                channel_moments(2)
                small_step(nc.vector.tensor_tensor(first_offset[:, 0:1], first_moments[:, 0:1], neg_shift[:, 0:1],
                                                   ALU.add))
                settle(0)
                small_step(nc.vector.scalar_tensor_tensor(out=first_offset[:, 1:2], in0=first_offset[:, 0:1],
                                                          scalar=first_offset[:, 0:1],
                                                          in1=first_moments[:, 1:2],
                                                          op0=ALU.mult, op1=ALU.add))
                settle(0)
                small_step(nc.vector.tensor_scalar(squares[:, 0, 0:1], first_offset[:, 1:2], float(H * W), None,
                                                   ALU.mult))
                settle(0)

            for n in range(8):
                merge(n)
            dve.wait_ge(stats_zero, 3)
            shift(0)
            for n in range(8, NC * W_BANKS):
                merge(n)
            channel_stats(1, range(STAT_PIECES))
            shift_chunk_0()
            dve.wait_ge(sizes_ready, NC)
            nc.vector.tensor_tensor(w_sizes, w_size[0], w_size[1], ALU.max).then_inc(max_step, 1)
            dve.wait_ge(max_step, 1)
            nc.vector.tensor_tensor(w_sizes_half, w_sizes[:, 0:9 * CH // 2], w_sizes[:, 9 * CH // 2:], ALU.max
                                    ).then_inc(max_step, 1)
            dve.wait_ge(max_step, 2)
            nc.vector.tensor_reduce(w_end[:], w_sizes_half, AX_X, ALU.max).then_inc(max_ready, 1)

            channel_stats(0, range(STAT_PIECES - 3))
            dve.wait_ge(max_all, 1)
            nc.vector.tensor_scalar(w_floor[:], w_max[:], 1e-30, None, ALU.max).then_inc(scale_step, 1)
            channel_stats(0, [STAT_PIECES - 3])
            dve.wait_ge(scale_step, 1)
            nc.vector.tensor_scalar(w_power[:].bitcast(U32), w_floor[:].bitcast(U32), 0x7F800000, None,
                                    ALU.bitwise_and).then_inc(scale_step, 1)
            channel_stats(0, [STAT_PIECES - 2])
            dve.wait_ge(scale_step, 2)
            nc.vector.reciprocal(w_inverse[:], w_power[:]).then_inc(scale_step, 1)
            channel_stats(0, [STAT_PIECES - 1])
            dve.wait_ge(scale_step, 3)
            nc.vector.tensor_scalar(w_scale[:], w_inverse[:], W_SCALE, None, ALU.mult
                                    ).then_inc(scale_ready, 1)

            def lo_w(n):
                c, j = W_ORDER[n]
                dve.wait_ge(whi_ready, n + 1)
                hi = w_hi[:, c, j, :, :].rearrange("p t n -> p (t n)")
                nc.vector.scalar_tensor_tensor(out=w_lo[:, c, j, :, :].rearrange("p t n -> p (t n)"), in0=g_tile(n),
                                               scalar=w_scale[:], in1=hi, op0=ALU.mult,
                                               op1=ALU.subtract).then_inc(wlo_ready, 1)

            squares_chunk_0()
            statistics(0, 0)
            lo_w(0)
            for c in range(NC):
                base(0, 0, c)
                transform(0, 0, c)
            for n in range(1, 4):
                lo_w(n)
            for j in range(NJ):
                nc.vector.tensor_scalar(evac_scale[:, j:j + 1], w_power[:],
                                        1.0 / (W_SCALE * X_SCALE * POINT_NORM[j]), None, ALU.mult
                                        ).then_inc(evac_ready, 1)
            round_pair(0, 0)
            transform_pair(0, 1)
            for n in range(4, len(W_ORDER)):
                lo_w(n)
            step(0, 0, NP, True)
            dve.wait_ge(last_pad_zero, 1)
            for s in range(1, 2 * IMG_PAIRS + 1):
                step(0, s, NP, True)
            with dve.Fori(1, NB // 2 - 1) as i:
                for s in range(1, 2 * IMG_PAIRS + 1):
                    step(i, s, NP, True)
            for s in range(1, 2 * IMG_PAIRS + 1):
                step(NB // 2 - 1, s, 2 * IMG_PAIRS - s, s < IMG_PAIRS)

        @block.tensor
        def _(pe):
            pe.wait_ge(lora_loaded, 32)
            for n in range(NC * W_BANKS):
                c, m = n // W_BANKS, n % W_BANKS
                if n >= 8:
                    pe.wait_ge(merged, n - 7)
                for tap in range(2 * m, min(2 * m + 2, 9)):
                    mm = nc.tensor.matmul(ps[:, n % 8, (tap % 2) * CH:(tap % 2 + 1) * CH],
                                          lora_a[:, tap, c * P:(c + 1) * P], lora_b, start=True, stop=True)
                mm.then_inc(delta_ready, 1)

            pe.wait_ge(pads_zero, 4)

            def product(s, k, co, w, hl, ci, first, last):
                for kw in range(TAPS):
                    for g in range(NG):
                        mm = nc.tensor.matmul(
                            plane(ps[:, 4 * k + 2 * co + g, 0:BANK]),
                            w[:, ci, PAIRS[s % NP][k], kw, co * P:(co + 1) * P],
                            u[:, s % U_SLOTS, ci, hl, g * BANK_TILES:(g + 1) * BANK_TILES, k, kw:kw + W],
                            start=(first and kw == 0), stop=(last and kw == TAPS - 1))
                return mm

            def multiply(Q, s):
                if isinstance(Q, int) and Q < NP:
                    pe.wait_ge(wlo_ready, 4 * (Q + 1))
                pe.wait_ge(lo_ready, NC * (Q + 1))
                for k in range(2):
                    for co in range(NC):
                        pe.wait_ge(prod_ready, PRODS * (Q - 1) + NC * k + co + 1)
                        for n, (w, hl) in enumerate(((w_hi, 0), (w_lo, 0), (w_hi, 1))):
                            for ci in range(NC):
                                mm = product(s, k, co, w, hl, ci, n + ci == 0, n == 2 and ci == NC - 1)
                        mm.then_inc(pe_done, 1)

            products = [(k, co) for k in range(2) for co in range(NC)]
            for ci in range(NC):
                pe.wait_ge(whi_ready, 2 * (ci + 1))
                pe.wait_ge(hi_ready, ci + 1)
                for k, co in products:
                    product(0, k, co, w_hi, 0, ci, ci == 0, False)
            for ci in range(NC):
                pe.wait_ge(wlo_ready, 2 * (ci + 1))
                for k, co in products:
                    product(0, k, co, w_lo, 0, ci, False, False)
            pe.wait_ge(lo_ready, NC)
            for k, co in products:
                for ci in range(NC):
                    mm = product(0, k, co, w_hi, 1, ci, False, ci == NC - 1)
                mm.then_inc(pe_done, 1)
            for s in range(1, IMG_PAIRS):
                multiply(s, s)
            with pe.Fori(1, NB) as b:
                for s in range(IMG_PAIRS):
                    multiply(IMG_PAIRS * b + s, s)


def kernel(x, L0_conv_W0, L0_conv_lora_A, L0_conv_lora_B):
    import numpy as np
    import concourse.bacc as bacc
    from concourse import mybir as mb
    from concourse.bass_utils import run_bass_kernel_spmd

    x = np.ascontiguousarray(x)
    w0t = np.ascontiguousarray(np.asarray(L0_conv_W0).transpose(1, 2, 3, 0).reshape(CH, 9, CH))
    lora_at = np.ascontiguousarray(np.asarray(L0_conv_lora_A).reshape(RANK, CH, 9).transpose(0, 2, 1))
    lora_bt = np.ascontiguousarray(np.asarray(L0_conv_lora_B).T)
    arrays = {"x_dram": x, "w0t_dram": w0t, "lora_at_dram": lora_at, "lora_bt_dram": lora_bt}
    nc = bacc.Bacc("TRN2", target_bir_lowering=False, num_devices=1)
    args = [nc.dram_tensor(name, a.shape, mb.dt.from_np(a.dtype), kind="ExternalInput").ap()
            for name, a in arrays.items()]
    out = nc.dram_tensor("out_dram", x.shape, mb.dt.from_np(x.dtype), kind="ExternalOutput").ap()
    build(nc, *args, out)
    r = run_bass_kernel_spmd(nc, [arrays], core_ids=[0])
    return r.results[0]["out_dram"]
```
